# Optimizing a Trainium2 kernel written in Bass

```python
import numpy as np
import jax
import jax.numpy as jnp

def _softmax(x, axis=-1):
    return jax.nn.softmax(x, axis=axis)

def _gelu(x):
    return jax.nn.gelu(x, approximate=True)

def _silu(x):
    return jax.nn.silu(x)

def _sigmoid(x):
    return jax.nn.sigmoid(x)

def _layernorm(x, axis=-1, eps=1e-05):
    m = jnp.mean(x, axis=axis, keepdims=True)
    v = jnp.var(x, axis=axis, keepdims=True)
    return (x - m) / jnp.sqrt(v + eps)

def _scatter_add(tgt, idx, src, axis=0):
    return tgt.at[idx].add(src)

def _segment_sum(src, seg, n):
    return jax.ops.segment_sum(src, seg, n)
kernel_name = 'mk_conv_attn_hybrid_d2_conv_nchw384_r2_262ab9'

def setup_inputs(seed: int=0):
    np.random.seed(seed)
    _w = jnp.asarray

    def _rec_inputs():
        import jax
        import jax.numpy as jnp
        _gk = jax.random.key(seed)
        x = -0.0004039 + 1 * jax.random.normal(jax.random.fold_in(_gk, 1), (32, 192, 32, 32), jnp.float32)
        return x
    x = _rec_inputs()

    def _L0_conv_setup():
        import jax, jax.numpy as jnp
        import numpy as np
        NUM_HEADS = 8
        EPS = 1e-12

        def _l2norm_tokens(t):
            n = jnp.sqrt(jnp.sum(t * t, axis=-1, keepdims=True))
            return t / jnp.maximum(n, EPS)
        key = jax.random.key(seed)
        ks = jax.random.split(key, 4)
        B, C, H, W = (32, 192, 32, 32)
        x = jax.random.normal(ks[0], (B, C, H, W), dtype=jnp.float32)
        w_qkv = jax.random.normal(ks[1], (3 * C, C), dtype=jnp.float32) * (1.0 / np.sqrt(C))
        b_qkv = jnp.zeros((3 * C,), dtype=jnp.float32)
        temperature = jnp.ones((NUM_HEADS, 1, 1), dtype=jnp.float32)
        w_proj = jax.random.normal(ks[2], (C, C), dtype=jnp.float32) * (1.0 / np.sqrt(C))
        b_proj = jnp.zeros((C,), dtype=jnp.float32)
        return {'x': x, 'w_qkv': w_qkv, 'b_qkv': b_qkv, 'temperature': temperature, 'w_proj': w_proj, 'b_proj': b_proj}
    _L0_conv_all = _L0_conv_setup()
    _L0_conv_in = {k: v for k, v in _L0_conv_all.items() if k in ('w_qkv', 'b_qkv', 'temperature', 'w_proj', 'b_proj')}
    del _L0_conv_all

    def _L1_attn_setup():
        import jax, jax.numpy as jnp
        import numpy as np
        NUM_HEADS = 6
        key = jax.random.key(seed)
        k1, k2, k3, k4 = jax.random.split(key, 4)
        B, T, C = (64, 128, 192)
        s = 1.0 / np.sqrt(C)
        return {'x': jax.random.normal(k1, (B, T, C), dtype=jnp.float32), 'Wq': jax.random.normal(k2, (C, C), dtype=jnp.float32) * s, 'Wk': jax.random.normal(k3, (C, C), dtype=jnp.float32) * s, 'Wv': jax.random.normal(k4, (C, C), dtype=jnp.float32) * s}
    _L1_attn_all = _L1_attn_setup()
    _L1_attn_in = {k: v for k, v in _L1_attn_all.items() if k in ('Wq', 'Wk', 'Wv')}
    del _L1_attn_all

    def _L1_ffn_setup():
        import jax, jax.numpy as jnp
        import numpy as np
        NUM_GROUPS = 5
        EPS = 1e-05
        QB = 128.0

        def _binarize_weights_groupwise(W):
            n_out = W.shape[0]
            gs = n_out // NUM_GROUPS
            Wb = jnp.zeros_like(W)
            for g in range(NUM_GROUPS):
                wg = W[g * gs:(g + 1) * gs]
                z = wg - wg.mean()
                ste = z + jax.lax.stop_gradient(jnp.sign(z) - z)
                Wb = Wb.at[g * gs:(g + 1) * gs].set(ste)
            return Wb

        def _quantize_activations_groupwise(x):
            n = x.shape[0]
            gs = n // NUM_GROUPS
            xq = jnp.zeros_like(x)
            for g in range(NUM_GROUPS):
                ag = x[g * gs:(g + 1) * gs]
                gamma = jnp.max(jnp.abs(ag))
                xq = xq.at[g * gs:(g + 1) * gs].set(jnp.clip(ag * QB / (gamma + EPS), -QB + EPS, QB - EPS))
            return xq

        def _bitlinear(x, W, b):
            Wb = _binarize_weights_groupwise(W)
            y = jnp.einsum('btc,oc->bto', x, Wb) + b
            return _quantize_activations_groupwise(y)
        key = jax.random.key(seed)
        k1, k2, k3, k4, k5 = jax.random.split(key, 5)
        B, T, C = (10, 1024, 192)
        H = 4 * C
        lim1 = 1.0 / np.sqrt(C)
        lim2 = 1.0 / np.sqrt(H)
        x = jax.random.normal(k1, (B, T, C), dtype=jnp.float32)
        W1 = jax.random.uniform(k2, (H, C), minval=-lim1, maxval=lim1, dtype=jnp.float32)
        b1 = jax.random.uniform(k3, (H,), minval=-lim1, maxval=lim1, dtype=jnp.float32)
        W2 = jax.random.uniform(k4, (C, H), minval=-lim2, maxval=lim2, dtype=jnp.float32)
        b2 = jax.random.uniform(k5, (C,), minval=-lim2, maxval=lim2, dtype=jnp.float32)
        return {'x': x, 'W1': W1, 'b1': b1, 'W2': W2, 'b2': b2}
    _L1_ffn_all = _L1_ffn_setup()
    _L1_ffn_in = {k: v for k, v in _L1_ffn_all.items() if k in ('W1', 'b1', 'W2', 'b2')}
    del _L1_ffn_all
    return {'x': x, 'L0_conv_w_qkv': _L0_conv_in['w_qkv'], 'L0_conv_b_qkv': _L0_conv_in['b_qkv'], 'L0_conv_temperature': _L0_conv_in['temperature'], 'L0_conv_w_proj': _L0_conv_in['w_proj'], 'L0_conv_b_proj': _L0_conv_in['b_proj'], 'L1_attn_Wq': _L1_attn_in['Wq'], 'L1_attn_Wk': _L1_attn_in['Wk'], 'L1_attn_Wv': _L1_attn_in['Wv'], 'L1_ffn_W1': _L1_ffn_in['W1'], 'L1_ffn_b1': _L1_ffn_in['b1'], 'L1_ffn_W2': _L1_ffn_in['W2'], 'L1_ffn_b2': _L1_ffn_in['b2']}

def reference(x, L0_conv_w_qkv, L0_conv_b_qkv, L0_conv_temperature, L0_conv_w_proj, L0_conv_b_proj, L1_attn_Wq, L1_attn_Wk, L1_attn_Wv, L1_ffn_W1, L1_ffn_b1, L1_ffn_W2, L1_ffn_b2):
    import jax
    import jax.numpy as jnp

    def _L0_conv_ref(x, w_qkv, b_qkv, temperature, w_proj, b_proj):
        import jax, jax.numpy as jnp
        import numpy as np
        NUM_HEADS = 8
        EPS = 1e-12

        def _l2norm_tokens(t):
            n = jnp.sqrt(jnp.sum(t * t, axis=-1, keepdims=True))
            return t / jnp.maximum(n, EPS)
        B, C, H, W = x.shape
        N = H * W
        nh = NUM_HEADS
        dh = C // nh
        xf = x.reshape(B, C, N)
        qkv = jnp.einsum('oc,bcn->bon', w_qkv, xf) + b_qkv[:, None]
        qkv = qkv.reshape(B, 3, nh, dh, N)
        q, k, v = (qkv[:, 0], qkv[:, 1], qkv[:, 2])
        q = _l2norm_tokens(q)
        k = _l2norm_tokens(k)
        attn = jnp.einsum('bhdn,bhen->bhde', q, k) * temperature
        attn = jax.nn.softmax(attn, axis=-1)
        out = jnp.einsum('bhde,bhen->bhdn', attn, v).reshape(B, C, N)
        out = jnp.einsum('oc,bcn->bon', w_proj, out) + b_proj[:, None]
        return x + out.reshape(B, C, H, W)

    def _L1_attn_ref(x, Wq, Wk, Wv):
        import jax, jax.numpy as jnp
        import numpy as np
        NUM_HEADS = 6
        B, T, C = x.shape
        H = NUM_HEADS
        d = C // H
        q = (x @ Wq).reshape(B, T, H, d)
        k = (x @ Wk).reshape(B, T, H, d)
        v = (x @ Wv).reshape(B, T, H, d)
        scale = 1.0 / jnp.sqrt(jnp.asarray(C, dtype=x.dtype))
        att = jnp.einsum('bqhd,bkhd->bhqk', q, k) * scale
        causal = jnp.tril(jnp.ones((T, T), dtype=bool))
        att = jnp.where(causal, att, -jnp.inf)
        att = jax.nn.softmax(att, axis=-1)
        out = jnp.einsum('bhqk,bkhd->bqhd', att, v)
        return out.reshape(B, T, C)

    def _L1_ffn_ref(x, W1, b1, W2, b2):
        import jax, jax.numpy as jnp
        import numpy as np
        NUM_GROUPS = 5
        EPS = 1e-05
        QB = 128.0

        def _binarize_weights_groupwise(W):
            n_out = W.shape[0]
            gs = n_out // NUM_GROUPS
            Wb = jnp.zeros_like(W)
            for g in range(NUM_GROUPS):
                wg = W[g * gs:(g + 1) * gs]
                z = wg - wg.mean()
                ste = z + jax.lax.stop_gradient(jnp.sign(z) - z)
                Wb = Wb.at[g * gs:(g + 1) * gs].set(ste)
            return Wb

        def _quantize_activations_groupwise(x):
            n = x.shape[0]
            gs = n // NUM_GROUPS
            xq = jnp.zeros_like(x)
            for g in range(NUM_GROUPS):
                ag = x[g * gs:(g + 1) * gs]
                gamma = jnp.max(jnp.abs(ag))
                xq = xq.at[g * gs:(g + 1) * gs].set(jnp.clip(ag * QB / (gamma + EPS), -QB + EPS, QB - EPS))
            return xq

        def _bitlinear(x, W, b):
            Wb = _binarize_weights_groupwise(W)
            y = jnp.einsum('btc,oc->bto', x, Wb) + b
            return _quantize_activations_groupwise(y)
        h = _bitlinear(x, W1, b1)
        h = jax.nn.gelu(h, approximate=False)
        out = _bitlinear(h, W2, b2)
        return out

    def _gn(v, G=32, eps=1e-05):
        B_, C_, H_, W_ = v.shape
        g = v.reshape(B_, G, C_ // G, H_, W_)
        m = jnp.mean(g, axis=(2, 3, 4), keepdims=True)
        s = jnp.var(g, axis=(2, 3, 4), keepdims=True)
        return ((g - m) / jnp.sqrt(s + eps)).reshape(v.shape)

    def _ln_c(v, eps=1e-06):
        m = jnp.mean(v, axis=1, keepdims=True)
        s = jnp.var(v, axis=1, keepdims=True)
        return (v - m) / jnp.sqrt(s + eps)

    def _ln_t(v, eps=1e-05):
        m = jnp.mean(v, axis=-1, keepdims=True)
        s = jnp.var(v, axis=-1, keepdims=True)
        return (v - m) / jnp.sqrt(s + eps)

    def _to_tokens(v):
        B_, C_, H_, W_ = v.shape
        return v.reshape(B_, C_, H_ * W_).transpose(0, 2, 1)

    def _from_tokens(t, like):
        B_, C_, H_, W_ = like.shape
        return t.transpose(0, 2, 1).reshape(B_, C_, H_, W_)
    x = _L0_conv_ref(x, L0_conv_w_qkv, L0_conv_b_qkv, L0_conv_temperature, L0_conv_w_proj, L0_conv_b_proj)
    t = _to_tokens(x)
    t = t + _L1_attn_ref(_ln_t(t), L1_attn_Wq, L1_attn_Wk, L1_attn_Wv)
    t = t + _L1_ffn_ref(_ln_t(t), L1_ffn_W1, L1_ffn_b1, L1_ffn_W2, L1_ffn_b2)
    x = _from_tokens(t, x)
    return x

_drawn_inputs = setup_inputs


def setup_inputs(seed=0):
    import zlib

    import numpy as np

    out = dict(_drawn_inputs(seed))
    spreads = {'L0_conv_b_qkv': (0.0, 0.452),
     'L0_conv_temperature': (1.0, 0.6),
     'L0_conv_b_proj': (0.0, 0.1)}
    factors = {'L1_ffn_b1': 8.0, 'L1_ffn_b2': 8.0}
    for name, (base, spread) in spreads.items():
        noise = np.random.default_rng([zlib.crc32(name.encode()), seed]).standard_normal(out[name].shape)
        drawn = base * np.exp(spread * noise) if base else spread * noise
        out[name] = jnp.asarray(drawn.astype(out[name].dtype))
    for name, factor in factors.items():
        out[name] = (out[name] * factor).astype(out[name].dtype)
    return out
```

```python
from contextlib import ExitStack

import numpy as np

import concourse.bass as bass
from concourse import mybir

F32 = mybir.dt.float32
F16 = mybir.dt.float16
BF16 = mybir.dt.bfloat16
ALU = mybir.AluOpType
ACT = mybir.ActivationFunctionType
AX = mybir.AxisListType
RMAX = bass.bass_isa.ReduceOp.max
RADD = bass.bass_isa.ReduceOp.add

P = 128
C = 192
CH = C // 2
NTOK = 1024
TT = NTOK // P
XH = 8
XD = C // XH
NH = 6
D = C // NH
HID = 4 * C
MH = HID // P
NGROUPS = 5
LN_EPS = 1e-5
Q_EPS = 1e-5
QB = 128.0
NORM_EPS2 = 1e-24
MASKED = -1e30
WTOP = 16.0

UNITS = NH * TT
TRIPLES = UNITS // 3
CHUNKS = [(n, c0, min(4, (n % 24) // 3 + 1 - c0)) for n in range(UNITS) for c0 in range(0, (n % 24) // 3 + 1, 4)]
PT_PER = len(CHUNKS) // 2
LAST_SLOT = 3 * (TRIPLES - 1) + 7
STEPS = ["xt0", "xt1", "xt2", "xt3", "g0", "g1", "wg0", "wg1", "na", "u", "mt", "t0", "t1", "t2", "t3",
         "z0", "z1", "z2", "z3", "qk0", "qk1", "qk2", "qk3", "qk4", "qk5", "v0", "v1", "v2", "v3"]
FREES = {"wg0": 2, "wg1": 2, "mt": 2}
FRONT_STEPS = len(STEPS)
FRONT_FREES = sum(FREES.get(s, 1) for s in STEPS)


def freed(step):
    return sum(FREES.get(s, 1) for s in STEPS[:STEPS.index(step) + 1])


SLOTS = {"xt0": 0, "xt1": 1, "xt2": 2, "xt3": 3, "g0a": 4, "g0": 5, "g1a": 6, "g1": 7, "wg0": 9, "wg1": 10,
         "na": 12, "u": 18, "mt": 20, "t0": 22, "t1": 23, "t2": 24, "t3": 25, "z0": 32, "z1": 33, "z2": 34,
         "z3": 35, "qk0": 36, "qk1": 37, "qk2": 38, "qk3": 39, "qk4": 40, "qk5": 41, "v0": 42, "v1": 43,
         "v2": 44, "v3": 45}
SMALL_SLOTS = {"norms": 13, "logits": 14, "xexp": 15, "attn": 16, "ln_stats": 26, "ln_norm": 29, "ln_lo": 30}


def hybrid_kernel(nc, x, wa, wb, wv, wpt, bp, temp, w3, w1, b1, w2, b2, out):
    B = x.shape[0]
    GS = B // NGROUPS
    assert GS % 2 == 0 and B - NGROUPS * GS == 2

    ctx = ExitStack()
    with ctx:
        def sb(name, shape, dt=F32):
            return ctx.enter_context(nc.sbuf_tensor(name, shape, dt))

        def sem(name):
            return ctx.enter_context(nc.semaphore(name))

        ident = sb("ident", [P, P])
        ident16 = sb("ident16", [P, P], F16)
        identb = sb("identb", [P, P], BF16)
        causal = sb("causal", [P, P], BF16)
        ones = sb("ones", [CH + 1, CH])
        epst = sb("epst", [P, TT])
        halfneg = sb("halfneg", [P, C + 2])
        WT = sb("WT", [CH + 1, 2, 2 * C])
        WV = sb("WV", [CH, 2, C + 1])
        WPT = sb("WPT", [CH, 2, C])
        IADD = sb("IADD", [CH + 1, 2, C])
        blockmask = sb("blockmask", [CH, 2, CH])
        tempc = sb("tempc", [CH, 2])
        W3h = sb("W3h", [P, 3, 3 * C], F16)
        W3l = sb("W3l", [P, 3, 3 * C], F16)
        W1b = sb("W1b", [P, 3, HID], F16)
        W2b = sb("W2b", [P, MH, C])
        B1 = sb("B1", [P, MH])
        B2 = sb("B2", [P, 2, C])
        sc = sb("sc", [P, 64])
        X = sb("X", [CH + 1, 2, NTOK])
        XT = sb("XT", [P, TT, C + 1])
        Z = XT[:, :, 0:C]
        zt = sb("zt", [P, 3, NTOK], F16)
        small = zt[:, :, :].rearrange("p a b -> p (a b)").bitcast(F32)
        G = small[0:CH + 1, 0:2 * (C + 1)].rearrange("p (a b) -> p a b", a=2)
        TK = small[0:CH + 1, 386:386 + 2 * C].rearrange("p (a b) -> p a b", a=2)
        U = small[0:CH, 770:770 + 2 * C].rearrange("p (a b) -> p a b", a=2)
        LOG = small[0:CH, 1154:1154 + 2 * CH].rearrange("p (a b) -> p a b", a=2)
        ATT = sb("ATT", [CH, 2, CH])
        NK = sb("NK", [CH, C + 2])
        MT = sb("MT", [CH + 1, 2, C])
        hi_z = sb("hi_z", [P, 3 * NTOK], F16)
        QKH = hi_z[:, :].rearrange("p (a b) -> p a b", a=3)
        zcat = hi_z[:, :].rearrange("p (a b) -> p a b", a=TT)
        PROD = hi_z[0:CH + 1, :].bitcast(F32)[:, 0:4 * C].rearrange("p (a b) -> p a b", a=2)
        T0 = sb("T0", [P, 2, TT, C])
        QS0 = sb("QS0", [P, NH, NTOK], F16)
        KS0 = sb("KS0", [P, NH, NTOK], F16)
        V0 = sb("V0", [P, TT, C])
        odd = sb("odd", [P, GS * 3 * NTOK if GS * 3 * NTOK > 18432 else 18432], F16)
        QS1 = odd[:, 0:6144].rearrange("p (a b) -> p a b", a=NH)
        KS1 = odd[:, 6144:12288].rearrange("p (a b) -> p a b", a=NH)
        QKL = odd[:, 12288:15360].rearrange("p (a b) -> p a b", a=3)
        V1 = odd[:, 15360:18432].bitcast(F32).rearrange("p (a b) -> p a b", a=TT)
        QS, KS, V = [QS0, QS1], [KS0, KS1], [V0, V1]
        Z2 = odd[:, 0:GS * 3 * NTOK].rearrange("p (b h j n) -> p b h j n", b=GS, h=2, j=3)
        Y2 = odd[:, 0:GS * 3 * NTOK].bitcast(F32).rearrange("p (b h n) -> p b h n", b=GS, h=2)
        T1 = sb("T1", [P, GS, TT, C])
        T1H = T1[:, :, :, :].rearrange("p b (h t) c -> p b h (t c)", h=2)
        work = sb("work", [P, 6144])
        PS = work[:, 0:2048].rearrange("p (a b) -> p a b", a=2)
        PTS = work[:, 2048:6144].rearrange("p (a b) -> p a b", a=4)
        H = work[:, :].rearrange("p (h m n) -> p h m n", h=2, m=MH)
        JUNK = work[:, 0:2048].rearrange("p (a b) -> p a b", a=4)
        OS = work[0:CH, 0:2048].rearrange("p (h c n) -> p h c n", h=2, c=2)
        OT = work[:, 2048:2048 + 2 * 4 * C].rearrange("p (h n) -> p h n", h=2)
        oT = sb("oT", [CH, 2, P])
        rowsum = sb("rowsum", [P, UNITS])
        nmax = sb("nmax", [P, UNITS])
        stats = sb("stats", [P, TT, 6])
        mv = sb("mv", [P, TT, 2])
        rstd = sb("rstd", [P, TT])
        fin = sb("fin", [P, CH])
        gm = sb("gm", [P, 16])
        scratch = T1[:, :, :, :].rearrange("p a b c -> p (a b c)")
        W3f = sb("W3f", [P, 3, 3 * C]) if GS < 6 else scratch[:, 0:1728].rearrange("p (a b) -> p a b", a=3)
        W1f = sb("W1f", [P, 3, HID]) if GS < 6 else scratch[:, 1728:4032].rearrange("p (a b) -> p a b", a=3)
        W1c = sb("W1c", [P, 3, HID]) if GS < 6 else scratch[:, 4032:6336].rearrange("p (a b) -> p a b", a=3)
        W2f = sb("W2f", [P, MH, C]) if GS < 6 else scratch[:, 6336:7488].rearrange("p (a b) -> p a b", a=MH)
        W2c = sb("W2c", [P, MH, C]) if GS < 6 else scratch[:, 7488:8640].rearrange("p (a b) -> p a b", a=MH)

        amax, wscale, vback = sc[:, 0:3], sc[:, 3:6], sc[:, 6:7]
        qkback, qkprod = sc[:, 7:8], sc[:, 8:9]
        sum1, sum2 = sc[:, 10:15], sc[:, 15:20]
        run1, run2, gam1, gam2 = sc[:, 20:21], sc[:, 21:22], sc[:, 22:23], sc[:, 23:24]
        ge, gr, r1, c1 = sc[:, 24:25], sc[:, 25:26], sc[:, 26:27], sc[:, 27:28]
        ge2, gr2, r2, c2, c2n = sc[:, 28:29], sc[:, 29:30], sc[:, 30:31], sc[:, 31:32], sc[:, 32:33]
        clip_hi, clip_lo, rb1 = sc[:, 33:39], sc[:, 39:45], sc[:, 45:51]
        rqt = sc[0:CH, 51:53]
        xmax, xsum = sc[0:CH, 53:55], sc[0:CH, 55:57]
        rsum3 = sc[:, 57:60]
        xrec = sc[0:CH, 60:62]
        half = sc[:, 62:63]

        S = ctx.enter_context(nc.psum_tensor("S", [P, 2, 1024], F32))
        PT = [ctx.enter_context(nc.psum_tensor(f"PT{i}", [P, 512], F32)) for i in range(2)]
        OUT = ctx.enter_context(nc.psum_tensor("OUT", [P, 512], F32))
        FR = ctx.enter_context(nc.psum_tensor("FR", [P, 512], F32))
        Y = [S[:, i // 2, 512 * (i % 2):512 * (i % 2) + 512] for i in range(4)]
        ZP = [FR, OUT]

        w_in = sem("w_in")
        bias_in = sem("bias_in")
        cst_made = sem("cst_made")
        prep = sem("prep")
        prep_all = sem("prep_all")
        w_ready = sem("w_ready")
        x_in = sem("x_in")
        front_full = sem("front_full")
        front_free = sem("front_free")
        norm2_made = sem("norm2_made")
        rnorm_made = sem("rnorm_made")
        xsoft = sem("xsoft")
        xexp_made = sem("xexp_made")
        ln_step = sem("ln_step")
        rstd_made = sem("rstd_made")
        zlo_made = sem("zlo_made")
        qkhi_made = sem("qkhi_made")
        qklo_made = sem("qklo_made")
        stacked = sem("stacked")
        scores_full = sem("scores_full")
        max_made = sem("max_made")
        exp_made = sem("exp_made")
        probs_read = sem("probs_read")
        pt_full = [sem(f"pt_full{i}") for i in range(2)]
        pt_free = [sem(f"pt_free{i}") for i in range(2)]
        pv_made = sem("pv_made")
        oT_made = sem("oT_made")
        o_back = sem("o_back")
        t1_step = sem("t1_step")
        ln2_step = sem("ln2_step")
        rstd2_made = sem("rstd2_made")
        z2lo_made = sem("z2lo_made")
        z2t_full = sem("z2t_full")
        z2t_made = sem("z2t_made")
        y1_full = sem("y1_full")
        abs_made = sem("abs_made")
        max1_step = sem("max1_step")
        gam1_made = sem("gam1_made")
        quant1_step = sem("quant1_step")
        y_full = sem("y_full")
        clip_made = sem("clip_made")
        gelu_made = sem("gelu_made")
        y2_full = sem("y2_full")
        y2_made = sem("y2_made")
        max2_step = sem("max2_step")
        gam2_made = sem("gam2_made")
        quant2_step = sem("quant2_step")
        o_step = sem("o_step")
        ot_full = sem("ot_full")
        os_made = sem("os_made")
        stored = sem("stored")
        passed = sem("passed")

        def groups(e, body, tail):
            with e.Fori(0, NGROUPS) as g:
                with e.Fori(0, GS // 2) as p:
                    body(e.snap(g * (GS // 2) + p), p)
                tail(g)

        LAST = NGROUPS * GS // 2

        def after(pair, u, per, n):
            return pair * (2 * per) + (u * per + n)

        def front_of(slot, run, parts):
            for name, at in parts:
                if at == slot:
                    run(name)

        def alone(e):
            e.sem_inc(passed, 1)

        block = ctx.enter_context(nc.Block())

        @block.sync
        def _(sp):
            for dst, src in ((WT[0:CH + 1, 0, :], wa), (WT[0:CH, 1, :], wb), (WV[:, :, :], wv), (WPT[:, :, :], wpt),
                             (tempc[:, :], temp), (W3f[:, :, :], w3), (W1f[:, :, :], w1), (B1[:, :], b1),
                             (W2f[:, :, :], w2), (B2[:, :, :], b2)):
                sp.dma_start(dst, src).then_inc(w_in, 16)
            sp.wait_ge(cst_made, 11)
            sp.dma_start(IADD[CH:CH + 1, 0, :], bp).then_inc(bias_in, 16)

            def load_x(b):
                sp.dma_start(X[0:CH, :, :], x[b].rearrange("(c p) n -> p c n", p=CH)).then_inc(x_in, 16)

            def front(pair, u, more):
                if more:
                    sp.wait_ge(front_full, after(pair, u, FRONT_STEPS, STEPS.index("t3") + 1))
                    load_x(pair * 2 + (u + 1))
                for m in range(3):
                    sp.wait_ge(qklo_made, after(pair, u, 6, 2 * m + 2))
                    for r in range(4):
                        i = 4 * m + r
                        stack = (QS if i < NH else KS)[u % 2]
                        srcs = (QKH, QKL, QKH, QKL) if i < NH else (QKH, QKH, QKL, QKL)
                        for part in range(4):
                            sp.dma_start(stack[32 * part:32 * part + 32, i % NH, :],
                                         srcs[part][32 * r:32 * r + 32, m, :]).then_inc(stacked, 16)

            def store(b, hf, n):
                sp.wait_ge(os_made, n)
                sp.dma_start(out[b].rearrange("(c p) n -> p c n", p=CH)[:, :, 512 * hf:512 * hf + 512],
                             OS[:, hf, :, :]).then_inc(stored, 16)

            sp.sem_inc(stored, 16)
            load_x(0)
            front(0, 0, True)

            def pair_body(pair, p):
                for u in range(2):
                    front(pair, u + 1, True)

            def group_tail(g):
                with sp.Fori(0, GS) as b:
                    for hf in range(2):
                        store(g * GS + b, hf, g * (2 * GS) + b * 2 + (hf + 1))

            groups(sp, pair_body, group_tail)
            front(LAST, 1, False)
            for u in range(2):
                for hf in range(2):
                    store(2 * LAST + u, hf, 4 * LAST + 2 * u + hf + 1)
            sp.wait_ge(stored, 16 * (2 * B + 1))

        @block.gpsimd
        def _(pool):
            pool.memset(ident[:, :], 0.0).then_inc(cst_made, 1)
            pool.memset(causal[:, :], 0.0).then_inc(cst_made, 1)
            pool.memset(IADD[:, :, :], 0.0).then_inc(cst_made, 1)
            pool.memset(blockmask[:, :, :], 0.0).then_inc(cst_made, 1)
            pool.memset(ones[:, :], 1.0).then_inc(cst_made, 1)
            pool.memset(halfneg[:, :], -0.5).then_inc(cst_made, 1)
            pool.memset(epst[:, :], LN_EPS).then_inc(cst_made, 1)
            pool.wait_ge(cst_made, 7)
            pool.affine_select(out=ident[:, :], in_=ident[:, :], compare_op=ALU.not_equal, fill=1.0, base=0,
                               pattern=[[-1, P]], channel_multiplier=1).then_inc(cst_made, 1)
            pool.affine_select(out=causal[:, :], in_=causal[:, :], compare_op=ALU.is_ge, fill=MASKED, base=0,
                               pattern=[[-1, P]], channel_multiplier=1).then_inc(cst_made, 1)
            pool.affine_select(out=IADD[0:CH, :, :], in_=IADD[0:CH, :, :], compare_op=ALU.not_equal, fill=1.0,
                               base=0, pattern=[[CH, 2], [-1, C]], channel_multiplier=1).then_inc(cst_made, 1)
            bm = blockmask[:, :, :].rearrange("p m (h d) -> p m h d", d=XD)
            pool.affine_select(out=bm, in_=bm, compare_op=ALU.is_ge, fill=MASKED, base=0,
                               pattern=[[0, 2], [-XD, CH // XD], [0, XD]], channel_multiplier=1).then_inc(cst_made, 1)
            pool.wait_ge(cst_made, 11)
            pool.affine_select(out=bm, in_=bm, compare_op=ALU.is_ge, fill=MASKED, base=XD - 1,
                               pattern=[[0, 2], [XD, CH // XD], [0, XD]], channel_multiplier=-1).then_inc(cst_made, 1)
            pool.tensor_copy(ident16[:, :], ident[:, :]).then_inc(cst_made, 1)
            pool.tensor_copy(identb[:, :], ident[:, :]).then_inc(cst_made, 1)
            pool.wait_ge(prep, 3)
            pool.partition_all_reduce(amax, sc[:, 33:36], P, RMAX).then_inc(prep_all, 1)
            pool.wait_ge(prep, 3 + 2 * NGROUPS)
            pool.partition_all_reduce(sc[:, 10:20], sc[:, 36:46], P, RADD).then_inc(prep_all, 1)
            pool.wait_ge(prep, 3 + 2 * NGROUPS + 3)
            pool.tensor_tensor(qkback, qkprod, half, ALU.pow).then_inc(prep_all, 1)

            def front(pair, u):
                pool.wait_ge(norm2_made, after(pair, u, 1, 1))
                pool.tensor_tensor(NK[:, :], NK[:, :], halfneg[0:CH, :], ALU.pow).then_inc(rnorm_made, 1)
                pool.wait_ge(ln_step, after(pair, u, 25, 16))
                pool.tensor_tensor(rstd[:, :], mv[:, :, 1], epst[:, :], ALU.add).then_inc(rstd_made, 1)
                pool.wait_ge(rstd_made, after(pair, u, 2, 1))
                pool.tensor_tensor(rstd[:, :], rstd[:, :], halfneg[:, 0:TT], ALU.pow).then_inc(rstd_made, 1)
                pool.wait_ge(ln_step, after(pair, u, 25, 25))
                pool.tensor_tensor(zcat[:, :, C:2 * C], Z, zcat[:, :, 0:C], ALU.subtract).then_inc(zlo_made, 1)

            front(0, 0)

            def pair_body(pair, p):
                for u in range(2):
                    front(pair, u + 1)

            def group_tail(g):
                with pool.Fori(0, GS) as b:
                    ab = pool.snap(g * GS + b)
                    pool.wait_ge(ln2_step, ab * 25 + 16)
                    pool.tensor_tensor(rstd[:, :], mv[:, :, 1], epst[:, :], ALU.add).then_inc(rstd2_made, 1)
                    pool.wait_ge(rstd2_made, ab * 2 + 1)
                    pool.tensor_tensor(rstd[:, :], rstd[:, :], halfneg[:, 0:TT], ALU.pow).then_inc(rstd2_made, 1)
                    pool.wait_ge(ln2_step, ab * 25 + 25)
                    pool.tensor_tensor(zcat[:, :, C:2 * C], Z, zcat[:, :, 0:C], ALU.subtract).then_inc(z2lo_made, 1)
                pool.wait_ge(max1_step, (g + 1) * (GS * 14 + 1))
                alone(pool)
                pool.partition_all_reduce(gam1, run1, P, RMAX).then_inc(gam1_made, 1)
                pool.wait_ge(max2_step, (g + 1) * (GS * 2 + 1))
                alone(pool)
                pool.partition_all_reduce(gam2, run2, P, RMAX).then_inc(gam2_made, 1)

            groups(pool, pair_body, group_tail)
            front(LAST, 1)

        @block.tensor
        def _(pe):
            mm = nc.tensor.matmul
            tr = nc.tensor.transpose
            pe.wait_ge(cst_made, 14)
            pe.wait_ge(w_in, 16 * 10)
            pe.wait_ge(w_ready, 1)

            def front_part(name, pair, u):
                f = u % 2
                last = None
                if name not in ("g0", "g1"):
                    step = {"g0a": "g0", "g1a": "g1"}.get(name, name)
                    n = freed(step) - FREES.get(step, 1)
                    if n or not isinstance(pair, int) or u:
                        pe.wait_ge(front_free, after(pair, u, FRONT_FREES, n))
                if name.startswith("xt"):
                    k = int(name[2:])
                    if k == 0:
                        pe.wait_ge(x_in, after(pair, u, 16, 16))
                    for t in range(2):
                        cols = slice((2 * k + t) * P, (2 * k + t + 1) * P)
                        o = t * (C + 1)
                        tr(FR[:, o:o + CH + 1], X[0:CH + 1, 0, cols], ident[0:CH + 1, 0:CH + 1])
                        last = tr(FR[:, o + CH + 1:o + C + 1], X[0:CH, 1, cols], ident[0:CH, 0:CH])
                elif name in ("g0a", "g0", "g1a", "g1"):
                    c0, m = (0, CH + 1) if name[1] == "0" else (CH + 1, CH)
                    o = 0
                    for t in (range(0, 4) if name.endswith("a") else range(4, 8)):
                        last = mm(FR[0:m, o:o + C + 1], XT[:, t, c0:c0 + m], XT[:, t, :],
                                  start=(t == 0), stop=(t == TT - 1))
                    if name.endswith("a"):
                        return
                elif name in ("wg0", "wg1"):
                    c0, m = (0, CH + 1) if name == "wg0" else (CH + 1, CH)
                    mm(FR[0:m, 0:2 * C], G[0:CH + 1, 0, c0:c0 + m], WT[0:CH + 1, 0, :], start=True, stop=False)
                    last = mm(FR[0:m, 0:2 * C], G[0:CH, 1, c0:c0 + m], WT[0:CH, 1, :], start=False, stop=True)
                elif name == "na":
                    for c, m in ((0, CH + 1), (1, CH)):
                        mm(FR[0:CH, 0:C], ones[0:m, :], PROD[0:m, c, C:2 * C], start=(c == 0), stop=(c == 1))
                    for j in range(2):
                        for c, m in ((0, CH + 1), (1, CH)):
                            mm(FR[0:CH, C + j:C + j + 1], PROD[0:m, c, CH * j:CH * j + CH], ones[0:m, 0:1],
                               start=(c == 0), stop=(c == 1))
                    for j in range(2):
                        for c, m in ((0, CH + 1), (1, CH)):
                            last = mm(FR[0:CH, 256 + CH * j:256 + CH * j + CH], WT[0:m, c, CH * j:CH * j + CH],
                                      TK[0:m, c, CH * j:CH * j + CH], start=(c == 0), stop=(c == 1))
                elif name == "u":
                    pe.wait_ge(xsoft, after(pair, u, 8, 8))
                    for j in range(2):
                        last = mm(FR[0:CH, C * j:C * j + C], ATT[:, j, :], WPT[:, j, :], start=True, stop=True)
                elif name == "mt":
                    for c, c0, m in ((0, 0, CH + 1), (1, CH + 1, CH)):
                        for j in range(2):
                            last = mm(FR[0:m, C * c:C * c + C], WV[:, j, c0:c0 + m], U[:, j, :],
                                      start=(j == 0), stop=(j == 1))
                elif name[0] == "t":
                    k = int(name[1:])
                    for t in range(2):
                        cols = slice((2 * k + t) * P, (2 * k + t + 1) * P)
                        mm(FR[:, C * t:C * t + C], X[0:CH + 1, 0, cols], MT[0:CH + 1, 0, :], start=True, stop=False)
                        last = mm(FR[:, C * t:C * t + C], X[0:CH, 1, cols], MT[0:CH, 1, :], start=False, stop=True)
                elif name[0] == "z":
                    k = int(name[1:])
                    if k == 0:
                        pe.wait_ge(zlo_made, after(pair, u, 1, 1))
                    last = turn_z(FR, k)
                elif name.startswith("qk"):
                    i = int(name[2:])
                    m, hf = i // 2, i % 2
                    for j in range(3):
                        for w in (W3h, W3l):
                            last = mm(FR[:, :], w[:, j, P * m:P * m + P], zt[:, j, 512 * hf:512 * hf + 512],
                                      start=(j == 0 and w is W3h), stop=(j == 2 and w is W3l))
                else:
                    k = int(name[1:])
                    for t in range(2):
                        for j in range(3):
                            for w in (W3h, W3l):
                                last = mm(FR[:, C * t:C * t + C], zt[:, j, (2 * k + t) * P:(2 * k + t + 1) * P],
                                          w[:, j, 2 * C:3 * C], start=(j == 0 and w is W3h),
                                          stop=(j == 2 and w is W3l))
                last.then_inc(front_full, 1)

            def turn_z(bank, k):
                v = bank[:, :].bitcast(F16).rearrange("p (j n) -> p j n", j=4)
                for t in range(2):
                    for j in range(3):
                        last = tr(v[:, j, P * t:P * t + P], zcat[:, 2 * k + t, P * j:P * j + P], ident16[:, :])
                return last

            pe.sem_inc(ot_full, 1)
            for name in SLOTS:
                front_part(name, 0, 0)

            def attention(pair, u, with_front):
                f = u % 2
                pe.wait_ge(stacked, after(pair, u, 48 * 16, 48 * 16))
                pe.wait_ge(front_free, after(pair, u, FRONT_FREES, FRONT_FREES))
                for n in range(LAST_SLOT + 1):
                    if n < UNITS:
                        h, qt = 3 * (n // 24) + n % 3, (n % 24) // 3
                        if n >= 2:
                            pe.wait_ge(exp_made, after(pair, u, UNITS, n - 1))
                        q = QS[f][:, h, P * qt:P * qt + P]
                        w = P * (qt + 1)
                        for c0 in range(0, w, 512):
                            c1_ = min(w, c0 + 512)
                            diag = c1_ == w
                            last = mm(S[:, n % 2, c0:c1_], q, KS[f][:, h, c0:c1_], start=True, stop=not diag)
                        last = mm(S[:, n % 2, w - P:w], identb[:, :], causal[:, :], start=False, stop=True)
                        last.then_inc(scores_full, 1)
                    m = n - 2
                    if 0 <= m < UNITS:
                        pe.wait_ge(exp_made, after(pair, u, UNITS, m + 1))
                        mine = [(i, c) for i, c in enumerate(CHUNKS) if c[0] == m]
                        for i, (_, c0, k) in mine:
                            if i >= 2:
                                pe.wait_ge(pt_free[i % 2], after(pair, u, PT_PER, i // 2))
                            for j in range(k):
                                last = tr(PT[i % 2][:, P * j:P * j + P], PS[:, m % 2, P * (c0 + j):P * (c0 + j) + P],
                                          ident[:, :])
                            last.then_inc(pt_full[i % 2], 1)
                        pe.wait_ge(pt_full[mine[-1][0] % 2], after(pair, u, PT_PER, mine[-1][0] // 2 + 1))
                        pe.sem_inc(probs_read, 1)
                    if n % 3 == 2 and n >= 5 and (n - 5) // 3 < TRIPLES:
                        k = (n - 5) // 3
                        done = [i for i, c in enumerate(CHUNKS) if c[0] <= 3 * k + 2]
                        for b in range(2):
                            pe.wait_ge(pt_free[b], after(pair, u, PT_PER, sum(i % 2 == b for i in done)))
                        if k >= 1:
                            pe.wait_ge(t1_step, after(pair, u, 3 * TRIPLES, 3 * (k - 1) + 2))
                        qt = (3 * k % 24) // 3
                        for j in range(qt + 1):
                            for hh in range(3):
                                h = 3 * (k // 8) + hh
                                last = mm(OUT[32 * hh:32 * hh + 32, 0:P],
                                          V[f][:, j, D * h:D * h + D], PTS[:, (3 * k + hh) % 4, P * j:P * j + P],
                                          start=(j == 0), stop=(j == qt), tile_position=(0, 32 * hh))
                        last.then_inc(pv_made, 1)
                    if n % 3 == 1 and n >= 7 and (n - 7) // 3 < TRIPLES:
                        k = (n - 7) // 3
                        pe.wait_ge(oT_made, after(pair, u, TRIPLES, k + 1))
                        tr(OUT[:, 256:256 + CH], oT[:, k % 2, :], ident[0:CH, 0:CH]).then_inc(o_back, 1)
                    if with_front:
                        front_of(n, lambda name: front_part(name, pair, u + 1), SLOTS.items())

            def ffn1(rhs, bank, i):
                for j in range(3):
                    last = mm(bank, W1b[:, j, P * (i % 6):P * (i % 6) + P], rhs[:, j, :],
                              start=(j == 0), stop=(j == 2))
                return last

            def turn_out(src, hf):
                for c in range(2):
                    for t in range(4):
                        o = 512 * c + P * t
                        last = tr(S[0:CH, hf, o:o + P], src(t, c), ident[:, :])
                return last

            def pair_body(pair, p):
                for u in range(2):
                    attention(pair, u, True)

            def group_tail(g):
                nb = g + 1
                pe.wait_ge(t1_step, nb * (GS * 3 * TRIPLES))
                pe.wait_ge(front_free, nb * (GS * FRONT_FREES) + FRONT_FREES)
                pe.wait_ge(stacked, nb * (GS * 48 * 16) + 48 * 16)
                alone(pe)
                with pe.Fori(0, GS) as b:
                    ab = pe.snap(g * GS + b)
                    pe.wait_ge(z2lo_made, ab + 1)
                    for k in range(4):
                        if k >= 2:
                            pe.wait_ge(z2t_made, ab * 4 + (k - 1))
                        turn_z(ZP[k % 2], k).then_inc(z2t_full, 1)
                    for i in range(12):
                        if i % 6 == 0:
                            pe.wait_ge(z2t_made, ab * 4 + (2 + 2 * (i // 6)))
                        if i >= 4:
                            pe.wait_ge(abs_made, ab * 12 + (i - 3))
                        ffn1(Z2[:, b, i // 6], Y[i % 4], i).then_inc(y1_full, 1)
                pe.wait_ge(abs_made, nb * (GS * 12))
                alone(pe)
                with pe.Fori(0, GS) as b:
                    ab = pe.snap(g * GS + b)
                    for i in range(12):
                        if i >= 4:
                            pe.wait_ge(clip_made, ab * 12 + (i - 3))
                        ffn1(Z2[:, b, i // 6], Y[i % 4], i).then_inc(y_full, 1)
                    for tp in range(4):
                        hf = tp // 2
                        pe.wait_ge(gelu_made, ab * 12 + 6 * (hf + 1))
                        if tp >= 2:
                            pe.wait_ge(y2_made, ab * 4 + (tp - 1))
                        for t in range(2):
                            o = P * (2 * (tp % 2) + t)
                            for m in range(MH):
                                last = mm(PT[tp % 2][:, C * t:C * t + C], H[:, hf, m, o:o + P], W2b[:, m, :],
                                          start=(m == 0), stop=(m == MH - 1))
                        last.then_inc(y2_full, 1)
                with pe.Fori(0, GS) as b:
                    ab = pe.snap(g * GS + b)
                    for hf in range(2):
                        pe.wait_ge(o_step, ab * 4 + (2 * hf + 2))
                        if hf == 1:
                            pe.wait_ge(os_made, ab * 2 + 1)
                        turn_out(lambda t, c: OT[:, hf, C * t + CH * c:C * t + CH * c + CH], hf).then_inc(ot_full, 1)
                pe.wait_ge(os_made, nb * (2 * GS))

            groups(pe, pair_body, group_tail)
            attention(LAST, 0, True)
            attention(LAST, 1, False)
            pe.wait_ge(t1_step, 3 * TRIPLES * B)
            for u in range(2):
                for hf in range(2):
                    if u:
                        pe.wait_ge(os_made, 4 * LAST + hf + 1)
                    turn_out(lambda t, c: T1[:, u, 4 * hf + t, CH * c:CH * c + CH], hf).then_inc(ot_full, 1)

        @block.scalar
        def _(act):
            A = nc.scalar.activation
            act.wait_ge(w_ready, 1)

            def front_part(name, pair, u):
                f = u % 2
                if name in ("g0a", "g1a", "na"):
                    return
                if name == "xexp":
                    act.wait_ge(xsoft, after(pair, u, 8, 5))
                    for j in range(2):
                        A(ATT[:, j, :], LOG[:, j, :], ACT.Exp, bias=xmax[:, j:j + 1],
                          accum_out=xsum[:, j:j + 1]).then_inc(xexp_made, 1)
                    return
                if name not in STEPS or name == "mt":
                    return
                act.wait_ge(front_full, after(pair, u, FRONT_STEPS, STEPS.index(name) + 1))
                if name.startswith("xt"):
                    k = int(name[2:])
                    o = A(XT[:, 2 * k:2 * k + 2, :], FR[:, 0:2 * (C + 1)].rearrange("p (t c) -> p t c", t=2), ACT.Copy)
                elif name in ("g0", "g1"):
                    c, m = int(name[1]), CH + 1 - int(name[1])
                    o = A(G[0:m, c, :], FR[0:m, 0:C + 1], ACT.Copy)
                elif name in ("wg0", "wg1"):
                    c, m = int(name[2]), CH + 1 - int(name[2])
                    act.wait_ge(front_free, after(pair, u, FRONT_FREES, freed(name) - 1))
                    o = A(TK[0:m, c, :], FR[0:m, C:2 * C], ACT.Copy)
                elif name == "u":
                    o = A(U[:, :, :], FR[0:CH, 0:2 * C].rearrange("p (a b) -> p a b", a=2), ACT.Copy)
                elif name[0] == "t":
                    k = int(name[1:])
                    o = A(T0[:, f, 2 * k:2 * k + 2, :], FR[:, 0:2 * C].rearrange("p (a b) -> p a b", a=2), ACT.Copy)
                elif name[0] == "z":
                    k = int(name[1:])
                    v = FR[:, :].bitcast(F16).rearrange("p (j n) -> p j n", j=4)
                    o = A(zt[:, :, 256 * k:256 * k + 256], v[:, 0:3, :], ACT.Copy)
                elif name.startswith("qk"):
                    i = int(name[2:])
                    A(QKH[:, i // 2, 512 * (i % 2):512 * (i % 2) + 512], FR[:, :], ACT.Copy,
                      scale=qkback).then_inc(qkhi_made, 1)
                    return
                else:
                    k = int(name[1:])
                    o = A(V[f][:, 2 * k:2 * k + 2, :], FR[:, 0:2 * C].rearrange("p (a b) -> p a b", a=2), ACT.Copy,
                          scale=vback)
                o.then_inc(front_free, 1)

            order = list(SLOTS.items()) + [("xexp", SMALL_SLOTS["xexp"])]
            order.sort(key=lambda a: a[1])
            for name, _ in order:
                front_part(name, 0, 0)

            def attention(pair, u, with_front):
                for n in range(LAST_SLOT + 1):
                    if n < UNITS:
                        act.wait_ge(max_made, after(pair, u, UNITS, n + 1))
                        if n >= 2:
                            act.wait_ge(probs_read, after(pair, u, UNITS, n - 1))
                        w = P * ((n % 24) // 3 + 1)
                        A(PS[:, n % 2, 0:w], S[:, n % 2, 0:w], ACT.Exp, bias=nmax[:, n:n + 1],
                          accum_out=rowsum[:, n:n + 1]).then_inc(exp_made, 1)
                    m = n - 2
                    for i, (m_, c0, k) in enumerate(CHUNKS):
                        if m_ == m and i % 4 == 3:
                            pt_copy(act, A, pair, u, i)
                    if n % 3 == 0 and n >= 6 and (n - 6) // 3 < TRIPLES:
                        k = (n - 6) // 3
                        act.wait_ge(pv_made, after(pair, u, TRIPLES, k + 1))
                        if k >= 2:
                            act.wait_ge(o_back, after(pair, u, TRIPLES, k - 1))
                        A(oT[:, k % 2, :], OUT[0:CH, 0:P], ACT.Copy).then_inc(oT_made, 1)
                    if with_front:
                        front_of(n, lambda name: front_part(name, pair, u + 1), order)

            def pt_copy(eng, copy, pair, u, i):
                m, c0, k = CHUNKS[i]
                eng.wait_ge(pt_full[i % 2], after(pair, u, PT_PER, i // 2 + 1))
                if m >= 4:
                    eng.wait_ge(pv_made, after(pair, u, TRIPLES, (m - 4) // 3 + 1))
                copy(PTS[:, m % 4, P * c0:P * (c0 + k)], PT[i % 2][:, 0:P * k], ACT.Copy).then_inc(pt_free[i % 2], 1)

            def put_out(hf, full):
                act.wait_ge(ot_full, full)
                A(OS[:, hf, :, :], S[0:CH, hf, :].rearrange("p (c n) -> p c n", c=2), ACT.Copy).then_inc(os_made, 1)

            def pair_body(pair, p):
                for u in range(2):
                    attention(pair, u, True)

            def group_tail(g):
                with act.Fori(0, GS) as b:
                    ab = act.snap(g * GS + b)
                    for i in range(12):
                        act.wait_ge(y1_full, ab * 12 + (i + 1))
                        if i >= 4:
                            act.wait_ge(max1_step, ab * 14 + g + (i - 3 + 1))
                        A(JUNK[:, i % 4, :], Y[i % 4], ACT.Abs, bias=B1[:, i % 6:i % 6 + 1]).then_inc(abs_made, 1)
                act.wait_ge(quant1_step, (g + 1) * 7)
                with act.Fori(0, GS) as b:
                    ab = act.snap(g * GS + b)
                    for i in range(12):
                        act.wait_ge(clip_made, ab * 12 + (i + 1))
                        h = H[:, i // 6, i % 6, :]
                        A(h, h, ACT.Gelu, bias=rb1[:, i % 6:i % 6 + 1], scale=r1).then_inc(gelu_made, 1)
                with act.Fori(0, GS) as b:
                    ab = act.snap(g * GS + b)
                    for hf in range(2):
                        if hf == 0:
                            act.wait_ge(stored, ab * 32 + 16)
                        put_out(hf, ab * 2 + (hf + 2))
                act.wait_ge(stored, (g + 1) * (GS * 32) + 16)

            groups(act, pair_body, group_tail)
            attention(LAST, 0, True)
            attention(LAST, 1, False)
            for u in range(2):
                act.wait_ge(stored, 16 * (4 * LAST + 2 * u + 1))
                for hf in range(2):
                    put_out(hf, 4 * LAST + 2 * u + hf + 2)

        @block.vector
        def _(dve):
            v = nc.vector
            dve.wait_ge(w_in, 16 * 10)
            for i in range(3):
                v.tensor_reduce(sc[:, 33 + i:34 + i], W3f[:, :, C * i:C * i + C], AX.XY, ALU.max,
                                apply_absolute_value=True).then_inc(prep, 1)
            g1 = HID // NGROUPS
            g2 = C // NGROUPS
            for g in range(NGROUPS):
                v.tensor_reduce(sc[:, 36 + g:37 + g], W1f[:, :, g1 * g:g1 * g + g1], AX.XY, ALU.add).then_inc(prep, 1)
            for g in range(NGROUPS):
                v.tensor_reduce(sc[:, 41 + g:42 + g], W2f[:, :, g2 * g:g2 * g + g2], AX.XY, ALU.add).then_inc(prep, 1)
            chain = [3 + 2 * NGROUPS]

            def link(ins):
                chain[0] += 1
                ins.then_inc(prep, 1)
                dve.wait_ge(prep, chain[0])

            dve.wait_ge(prep_all, 1)
            v.memset(half, 0.5).then_inc(prep, 1)
            chain[0] += 1
            v.tensor_scalar(amax, amax, 1e-18, None, ALU.max).then_inc(prep, 1)
            chain[0] += 1
            dve.wait_ge(prep, chain[0])
            link(v.tensor_scalar(qkprod, amax[:, 0:1], amax[:, 1:2], 1.0 / (WTOP * WTOP * float(np.sqrt(C))),
                                 ALU.mult, ALU.mult))
            link(v.reciprocal(wscale, amax))
            link(v.tensor_scalar(wscale, wscale, WTOP, None, ALU.mult))
            link(v.tensor_scalar(vback, amax[:, 2:3], 1.0 / WTOP, None, ALU.mult))
            for i in range(3):
                link(v.tensor_scalar(W3f[:, :, C * i:C * i + C], W3f[:, :, C * i:C * i + C], wscale[:, i:i + 1], None,
                                     ALU.mult))
            link(v.tensor_copy(W3h[:, :, :], W3f[:, :, :]))
            link(v.tensor_tensor(W3l[:, :, :], W3f[:, :, :], W3h[:, :, :], ALU.subtract))
            dve.wait_ge(prep_all, 2)
            link(v.tensor_scalar(sum1, sum1, 1.0 / (2 * g1 * C), None, ALU.mult))
            link(v.tensor_scalar(sum2, sum2, 1.0 / (g2 * HID), None, ALU.mult))
            link(v.memset(W1b[:, :, :], 0.0))
            link(v.memset(W2b[:, :, :], 0.0))
            for wf, wc, wbin, gs, means in ((W1f, W1c, W1b, g1, sum1), (W2f, W2c, W2b, g2, sum2)):
                for g in range(NGROUPS):
                    cols = slice(gs * g, gs * g + gs)
                    link(v.tensor_scalar(wc[:, :, cols], wf[:, :, cols], means[:, g:g + 1], None, ALU.is_lt))
                    link(v.scalar_tensor_tensor(out=wbin[:, :, cols], in0=wf[:, :, cols], scalar=means[:, g:g + 1],
                                                in1=wc[:, :, cols], op0=ALU.is_gt, op1=ALU.subtract))
            dve.wait_ge(prep_all, 3)
            dve.wait_ge(cst_made, 14)
            dve.wait_ge(bias_in, 16)
            v.memset(X[CH:CH + 1, 0, :], 1.0).then_inc(w_ready, 1)

            def layer_norm(src, step, step_base, rs_sem, rs_value, part):
                if part == "stats":
                    for t in range(TT):
                        v.bn_stats(stats[:, t, :], src(t)).then_inc(step, 1)
                    for t in range(TT):
                        dve.wait_ge(step, step_base + (t + 1))
                        alone(dve)
                        v.bn_aggr(mv[:, t, :], stats[:, t, :]).then_inc(step, 1)
                else:
                    dve.wait_ge(rs_sem, rs_value)
                    for t in range(TT):
                        v.tensor_scalar(Z[:, t, :], src(t), mv[:, t, 0:1], rstd[:, t:t + 1], ALU.subtract,
                                        ALU.mult).then_inc(step, 1)
                    dve.wait_ge(step, step_base + 24)
                    v.tensor_copy(zcat[:, :, 0:C], Z).then_inc(step, 1)

            def front_part(name, pair, u):
                f = u % 2
                if name in ("wg0", "wg1"):
                    c, m = int(name[2]), CH + 1 - int(name[2])
                    dve.wait_ge(front_full, after(pair, u, FRONT_STEPS, STEPS.index(name) + 1))
                    v.tensor_tensor(PROD[0:m, c, :], FR[0:m, 0:2 * C], WT[0:m, c, :], ALU.mult).then_inc(front_free, 1)
                elif name == "norms":
                    dve.wait_ge(front_full, after(pair, u, FRONT_STEPS, STEPS.index("na") + 1))
                    v.tensor_scalar(NK[:, :], FR[0:CH, 0:C + 2], NORM_EPS2, None, ALU.max).then_inc(norm2_made, 1)
                elif name == "logits":
                    dve.wait_ge(rnorm_made, after(pair, u, 1, 1))
                    v.tensor_tensor(rqt, NK[:, C:C + 2], tempc[:, :], ALU.mult).then_inc(xsoft, 1)
                    dve.wait_ge(xsoft, after(pair, u, 8, 1))
                    for j in range(2):
                        o = v.scalar_tensor_tensor(out=LOG[:, j, :], in0=FR[0:CH, 256 + CH * j:256 + CH * j + CH],
                                                   scalar=rqt[:, j:j + 1], in1=NK[:, CH * j:CH * j + CH],
                                                   op0=ALU.mult, op1=ALU.mult).then_inc(xsoft, 1)
                    dve.wait_ge(xsoft, after(pair, u, 8, 3))
                    dve.sem_inc(front_free, 1)
                    v.tensor_tensor(LOG, LOG, blockmask[:, :, :], ALU.add).then_inc(xsoft, 1)
                    dve.wait_ge(xsoft, after(pair, u, 8, 4))
                    v.tensor_reduce(xmax, LOG, AX.X, ALU.max, negate=True).then_inc(xsoft, 1)
                elif name == "attn":
                    dve.wait_ge(xexp_made, after(pair, u, 2, 2))
                    v.reciprocal(xrec, xsum).then_inc(xsoft, 1)
                    dve.wait_ge(xsoft, after(pair, u, 8, 6))
                    for j in range(2):
                        v.tensor_scalar(ATT[:, j, :], ATT[:, j, :], xrec[:, j:j + 1], None,
                                        ALU.mult).then_inc(xsoft, 1)
                elif name == "mt":
                    dve.wait_ge(front_full, after(pair, u, FRONT_STEPS, STEPS.index("mt") + 1))
                    for c in range(2):
                        m = CH + 1 - c
                        v.tensor_tensor(MT[0:m, c, :], FR[0:m, C * c:C * c + C], IADD[0:m, c, :],
                                        ALU.add).then_inc(front_free, 1)
                elif name in ("ln_stats", "ln_norm"):
                    if name == "ln_stats":
                        dve.wait_ge(front_free, after(pair, u, FRONT_FREES, freed("t3")))
                    layer_norm(lambda t: T0[:, f, t, :], ln_step, after(pair, u, 25, 0), rstd_made,
                               after(pair, u, 2, 2), name[3:])
                elif name.startswith("qk"):
                    i = int(name[2:])
                    dve.wait_ge(qkhi_made, after(pair, u, 6, i + 1))
                    cols = slice(512 * (i % 2), 512 * (i % 2) + 512)
                    v.scalar_tensor_tensor(out=QKL[:, i // 2, cols], in0=FR[:, :], scalar=qkback,
                                           in1=QKH[:, i // 2, cols], op0=ALU.mult,
                                           op1=ALU.subtract).then_inc(qklo_made, 1)
                    dve.wait_ge(qklo_made, after(pair, u, 6, i + 1))
                    dve.sem_inc(front_free, 1)

            order = list(SLOTS.items()) + [a for a in SMALL_SLOTS.items() if a[0] not in ("xexp", "ln_lo")]
            order.sort(key=lambda a: a[1])
            for name, _ in order:
                front_part(name, 0, 0)

            def attention(pair, u, with_front, slot):
                f = u % 2
                for n in range(LAST_SLOT + 1):
                    if n < UNITS:
                        dve.wait_ge(scores_full, after(pair, u, UNITS, n + 1))
                        w = P * ((n % 24) // 3 + 1)
                        v.tensor_reduce(nmax[:, n:n + 1], S[:, n % 2, 0:w], AX.X, ALU.max,
                                        negate=True).then_inc(max_made, 1)
                    for i, (m, c0, k) in enumerate(CHUNKS):
                        if m == n - 2 and i % 4 != 3:
                            dve.wait_ge(pt_full[i % 2], after(pair, u, PT_PER, i // 2 + 1))
                            if m >= 4:
                                dve.wait_ge(pv_made, after(pair, u, TRIPLES, (m - 4) // 3 + 1))
                            v.tensor_copy(PTS[:, m % 4, P * c0:P * (c0 + k)],
                                          PT[i % 2][:, 0:P * k]).then_inc(pt_free[i % 2], 1)
                    if n % 3 == 1 and n >= 7 and (n - 7) // 3 < TRIPLES:
                        k = (n - 7) // 3
                        base = after(pair, u, 3 * TRIPLES, 3 * k)
                        dve.wait_ge(o_back, after(pair, u, TRIPLES, k + 1))
                        v.reciprocal(rsum3, rowsum[:, 3 * k:3 * k + 3]).then_inc(t1_step, 1)
                        dve.wait_ge(t1_step, base + 1)
                        v.tensor_tensor(fin[:, :].rearrange("p (h d) -> p h d", h=3),
                                        OUT[:, 256:256 + CH].rearrange("p (h d) -> p h d", h=3),
                                        rsum3[:, 0:3].unsqueeze(2).broadcast_to([P, 3, D]), ALU.mult).then_inc(t1_step, 1)
                        dve.wait_ge(t1_step, base + 2)
                        qt, cols = k % 8, slice(CH * (k // 8), CH * (k // 8) + CH)
                        v.tensor_tensor(T1[:, slot, qt, cols], fin[:, :], T0[:, f, qt, cols],
                                        ALU.add).then_inc(t1_step, 1)
                    if with_front:
                        front_of(n, lambda name: front_part(name, pair, u + 1), order)

            def pair_body(pair, p):
                for u in range(2):
                    attention(pair, u, True, p * 2 + u)

            def group_tail(g):
                nb = g + 1
                dve.wait_ge(stacked, nb * (GS * 48 * 16) + 48 * 16)
                v.memset(run1, 0.0).then_inc(max1_step, 1)
                with dve.Fori(0, GS) as b:
                    ab = dve.snap(g * GS + b)
                    for part in ("stats", "norm"):
                        layer_norm(lambda t: T1[:, b, t, :], ln2_step, ab * 25, rstd2_made, ab * 2 + 2, part)
                    for k in range(4):
                        dve.wait_ge(z2t_full, ab * 4 + (k + 1))
                        zv = ZP[k % 2][:, :].bitcast(F16).rearrange("p (j n) -> p j n", j=4)
                        v.tensor_scalar(Z2[:, b, k // 2, :, 256 * (k % 2):256 * (k % 2) + 256], zv[:, 0:3, :], 1.0,
                                        None, ALU.mult).then_inc(z2t_made, 1)
                    base = ab * 14 + (g + 1)
                    for i in range(12):
                        dve.wait_ge(abs_made, ab * 12 + (i + 1))
                        v.tensor_reduce(gm[:, i:i + 1], JUNK[:, i % 4, :], AX.X, ALU.max).then_inc(max1_step, 1)
                    dve.wait_ge(max1_step, base + 12)
                    v.tensor_reduce(gm[:, 12:13], gm[:, 0:12], AX.X, ALU.max).then_inc(max1_step, 1)
                    dve.wait_ge(max1_step, base + 13)
                    v.tensor_tensor(run1, run1, gm[:, 12:13], ALU.max).then_inc(max1_step, 1)
                dve.wait_ge(gam1_made, nb)
                q0 = g * 7
                v.tensor_scalar(ge, gam1, Q_EPS, None, ALU.add).then_inc(quant1_step, 1)
                dve.wait_ge(quant1_step, q0 + 1)
                v.reciprocal(gr, ge).then_inc(quant1_step, 1)
                v.tensor_scalar(c1, ge, (QB - Q_EPS) / QB, None, ALU.mult).then_inc(quant1_step, 1)
                dve.wait_ge(quant1_step, q0 + 2)
                v.tensor_scalar(r1, gr, QB, None, ALU.mult).then_inc(quant1_step, 1)
                dve.wait_ge(quant1_step, q0 + 4)
                v.tensor_scalar(clip_hi, B1[:, :], -1.0, c1, ALU.mult, ALU.add).then_inc(quant1_step, 1)
                v.tensor_scalar(clip_lo, B1[:, :], -1.0, c1, ALU.mult, ALU.subtract).then_inc(quant1_step, 1)
                v.tensor_scalar(rb1, B1[:, :], r1, None, ALU.mult).then_inc(quant1_step, 1)
                dve.wait_ge(quant1_step, q0 + 7)
                v.memset(run2, 0.0).then_inc(max2_step, 1)
                with dve.Fori(0, GS) as b:
                    ab = dve.snap(g * GS + b)
                    for i in range(12):
                        dve.wait_ge(y_full, ab * 12 + (i + 1))
                        v.tensor_scalar(H[:, i // 6, i % 6, :], Y[i % 4], clip_hi[:, i % 6:i % 6 + 1],
                                        clip_lo[:, i % 6:i % 6 + 1], ALU.min, ALU.max).then_inc(clip_made, 1)
                    for tp in range(4):
                        dve.wait_ge(y2_full, ab * 4 + (tp + 1))
                        o = 2 * C * (tp % 2)
                        v.tensor_tensor(Y2[:, b, tp // 2, o:o + 2 * C], PT[tp % 2][:, 0:2 * C],
                                        B2[:, :, :].rearrange("p a c -> p (a c)"), ALU.add).then_inc(y2_made, 1)
                    base = ab * 2 + (g + 1)
                    dve.wait_ge(y2_made, ab * 4 + 4)
                    alone(dve)
                    v.tensor_reduce(gm[:, 13:14], Y2[:, b], AX.XY, ALU.max,
                                    apply_absolute_value=True).then_inc(max2_step, 1)
                    dve.wait_ge(max2_step, base + 1)
                    v.tensor_tensor(run2, run2, gm[:, 13:14], ALU.max).then_inc(max2_step, 1)
                dve.wait_ge(gam2_made, nb)
                q0 = g * 5
                v.tensor_scalar(ge2, gam2, Q_EPS, None, ALU.add).then_inc(quant2_step, 1)
                dve.wait_ge(quant2_step, q0 + 1)
                v.reciprocal(gr2, ge2).then_inc(quant2_step, 1)
                v.tensor_scalar(c2, ge2, (QB - Q_EPS) / QB, None, ALU.mult).then_inc(quant2_step, 1)
                v.tensor_scalar(c2n, ge2, -(QB - Q_EPS) / QB, None, ALU.mult).then_inc(quant2_step, 1)
                dve.wait_ge(quant2_step, q0 + 4)
                v.tensor_scalar(r2, gr2, QB, None, ALU.mult).then_inc(quant2_step, 1)
                dve.wait_ge(quant2_step, q0 + 5)
                alone(dve)
                with dve.Fori(0, GS) as b:
                    ab = dve.snap(g * GS + b)
                    for hf in range(2):
                        dve.wait_ge(ot_full, ab * 2 + 1)
                        v.tensor_scalar(OT[:, hf, :], Y2[:, b, hf, :], c2, c2n, ALU.min, ALU.max).then_inc(o_step, 1)
                        dve.wait_ge(o_step, ab * 4 + (2 * hf + 1))
                        v.scalar_tensor_tensor(out=OT[:, hf, :], in0=OT[:, hf, :], scalar=r2, in1=T1H[:, b, hf, :],
                                               op0=ALU.mult, op1=ALU.add).then_inc(o_step, 1)

            groups(dve, pair_body, group_tail)
            attention(LAST, 0, True, 0)
            attention(LAST, 1, False, 1)


def kernel(x, L0_conv_w_qkv, L0_conv_b_qkv, L0_conv_temperature, L0_conv_w_proj, L0_conv_b_proj, L1_attn_Wq,
           L1_attn_Wk, L1_attn_Wv, L1_ffn_W1, L1_ffn_b1, L1_ffn_W2, L1_ffn_b2):
    import concourse.bacc as bacc
    from concourse.bass_utils import run_bass_kernel_spmd as run

    (x, wqkv, bqkv, temp, wp, bp, wq, wk, wv, w1, b1, w2, b2) = [np.asarray(a) for a in (
        x, L0_conv_w_qkv, L0_conv_b_qkv, L0_conv_temperature, L0_conv_w_proj, L0_conv_b_proj, L1_attn_Wq,
        L1_attn_Wk, L1_attn_Wv, L1_ffn_W1, L1_ffn_b1, L1_ffn_W2, L1_ffn_b2)]
    B = x.shape[0]
    wt = wqkv.T
    stack = lambda a: np.concatenate([a, a], 0).reshape(3, P, -1).transpose(1, 0, 2)
    v_rows, v_bias = wqkv[2 * C:3 * C], bqkv[2 * C:3 * C][:, None]
    arrays = {
        "x": x.reshape(B, C, NTOK),
        "wa": np.concatenate([wt[0:CH, 0:2 * C], bqkv[None, 0:2 * C]], 0),
        "wb": wt[CH:C, 0:2 * C],
        "wv": np.concatenate([v_rows[:, 0:CH], v_bias, v_rows[:, CH:C]], 1).reshape(2, CH, C + 1).transpose(1, 0, 2),
        "wpt": wp.T.reshape(2, CH, C).transpose(1, 0, 2),
        "bp": bp[None, :],
        "temp": np.repeat(temp.reshape(XH), XD).reshape(2, CH).T,
        "w3": stack(np.concatenate([wq, wk, wv], 1)),
        "w1": stack(w1.T),
        "b1": b1.reshape(MH, P).T,
        "w2": w2.T.reshape(MH, P, C).transpose(1, 0, 2),
        "b2": np.broadcast_to(b2, (P, 2, C)),
    }
    arrays = {f"in_{k}": np.ascontiguousarray(a) for k, a in arrays.items()}
    nc = bacc.Bacc("TRN2", target_bir_lowering=False, num_devices=1)
    args = [nc.dram_tensor(k, a.shape, F32, kind="ExternalInput").ap() for k, a in arrays.items()]
    out = nc.dram_tensor("out_y", (B, C, NTOK), F32, kind="ExternalOutput").ap()
    hybrid_kernel(nc, *args, out)
    r = run(nc, [arrays], core_ids=[0])
    return r.results[0]["out_y"].reshape(x.shape)
```

```python
from contextlib import ExitStack

import numpy as np

import concourse.bass as bass
from concourse import mybir

F32 = mybir.dt.float32
F16 = mybir.dt.float16
BF16 = mybir.dt.bfloat16
ALU = mybir.AluOpType
ACT = mybir.ActivationFunctionType
AX = mybir.AxisListType
RMAX = bass.bass_isa.ReduceOp.max
RADD = bass.bass_isa.ReduceOp.add

P = 128
C = 192
CH = C // 2
NTOK = 1024
TT = NTOK // P
XH = 8
XD = C // XH
NH = 6
D = C // NH
HID = 4 * C
MH = HID // P
NGROUPS = 5
LN_EPS = 1e-5
Q_EPS = 1e-5
QB = 128.0
NORM_EPS2 = 1e-24
MASKED = -1e30
WTOP = 16.0

UNITS = NH * TT
U2 = 2 * UNITS
K2 = U2 // 3
TILES = [(0, 7), (1, 6), (2, 5), (3, 4)]
AHEAD = 2
PV_AT, OT_AT, BACK_AT = (7, 9), (8, 10), (9, 11)
LAST_SLOT = 6 * (K2 // 2 - 1) + BACK_AT[1]
RING = 4
STACKS = 8 * 16


def qtile(n):
    return TILES[n // 6 % 4][n % 2]


def triple_of(n):
    return 2 * (n // 6) + n % 2


def unit_of(k, hh):
    return 6 * (k // 2) + k % 2 + 2 * hh


def triples_at(slot, at):
    return [k for k in range(K2) if 6 * (k // 2) + at[k % 2] == slot]


def transposed():
    out = []
    for slot in range(LAST_SLOT + 1):
        m = slot - AHEAD
        if 0 <= m < U2:
            out += [(slot, "p", m, c0, min(4, qtile(m) + 1 - c0)) for c0 in range(0, qtile(m) + 1, 4)]
        out += [(slot, "o", k, 0, 0) for k in triples_at(slot, BACK_AT)]
    return out


CHUNKS = transposed()
PT_PER = len(CHUNKS) // 2
assert len(CHUNKS) % 2 == 0
STEPS = ["xt0", "xt1", "xt2", "xt3", "g0", "g1", "wg0", "wg1", "na", "rb", "u", "mt", "t0", "t1", "t2", "t3",
         "z0", "z1", "z2", "z3", "qk0", "qk1", "qk2", "qk3", "qk4", "qk5", "v0", "v1", "v2", "v3"]
FREES = {"wg0": 2, "wg1": 2, "mt": 2}
XSOFT = 9
FRONT_STEPS = len(STEPS)
NEEDS = {"g0": "xt3", "wg0": "g1", "na": "wg1", "mt": "u", "t0": "mt", "qk0": "z3"}


def bank_of(step):
    return STEPS.index(step) % 2


def freed(step):
    i = STEPS.index(step)
    return sum(FREES.get(s, 1) for s in STEPS[i % 2:i + 1:2])


FRONT_FREES = [freed(STEPS[-2]), freed(STEPS[-1])]
assert FRONT_STEPS % 2 == 0


SLOTS = {"xt0": 0, "xt1": 1, "xt2": 2, "xt3": 3, "g0a": 4, "g0": 5, "g1a": 6, "g1": 7, "wg0": 9, "wg1": 10,
         "na": 11, "rb": 14, "u": 17, "mt": 18, "t0": 19, "t1": 20, "t2": 21, "t3": 22, "z0": 28, "z1": 29,
         "z2": 30, "z3": 31, "qk0": 32, "qk1": 33, "qk2": 34, "qk3": 35, "qk4": 36, "qk5": 37, "v0": 38, "v1": 39,
         "v2": 40, "v3": 41}
SMALL_SLOTS = {"norms": 12, "rdiag": 13, "logits": 15, "xexp": 16, "attn": 16.5, "ln_stats": 23, "ln_norm": 25}


def hybrid_kernel(nc, x, wa, wb, wv, wpt, bp, temp, w3, w1, b1, w2, b2, out):
    B = x.shape[0]
    GS = B // NGROUPS
    assert GS % 2 == 0 and B - NGROUPS * GS == 2

    ctx = ExitStack()
    with ctx:
        def sb(name, shape, dt=F32):
            return ctx.enter_context(nc.sbuf_tensor(name, shape, dt))

        def sem(name):
            return ctx.enter_context(nc.semaphore(name))

        ident = sb("ident", [P, P])
        ident16 = sb("ident16", [P, P], F16)
        identb = sb("identb", [P, P], BF16)
        causal = sb("causal", [P, P], BF16)
        ones = sb("ones", [CH + 1, CH])
        epst = sb("epst", [P, TT])
        halfneg = sb("halfneg", [P, TT])
        WT = sb("WT", [CH + 1, 2, 2 * C])
        WV = sb("WV", [CH, 2, C + 1])
        WPT = sb("WPT", [CH, 2, C])
        IADD = sb("IADD", [CH + 1, 2, C])
        blockmask = sb("blockmask", [CH, 2, CH])
        tempc = sb("tempc", [CH, 2])
        W3h = sb("W3h", [P, 3, 3 * C], F16)
        W3l = sb("W3l", [P, 3, 3 * C], F16)
        W1b = sb("W1b", [P, 3, HID], F16)
        W2b = sb("W2b", [P, MH, C])
        B1 = sb("B1", [P, MH])
        B2 = sb("B2", [P, C])
        sc = sb("sc", [P, 64])
        X = sb("X", [CH + 1, 2, NTOK])
        XT = sb("XT", [P, TT, C + 1])
        Z = XT[:, :, 0:C]
        zt = sb("zt", [P, 3, NTOK], F16)
        small = zt[:, :, :].rearrange("p a b -> p (a b)").bitcast(F32)
        G = small[0:CH + 1, 0:2 * (C + 1)].rearrange("p (a b) -> p a b", a=2)
        TK = small[0:CH + 1, 386:386 + 2 * C].rearrange("p (a b) -> p a b", a=2)
        U = small[0:CH, 770:770 + 2 * C].rearrange("p (a b) -> p a b", a=2)
        LOG = small[0:CH, 1154:1154 + 2 * CH].rearrange("p (a b) -> p a b", a=2)
        NK = sb("NK", [CH, 4])
        RD = sb("RD", [CH, 2, CH])
        ATT = RD
        MT = sb("MT", [CH + 1, 2, C])
        hi_z = sb("hi_z", [P, 3 * NTOK], F16)
        QKH = hi_z[:, :].rearrange("p (a b) -> p a b", a=3)
        zcat = hi_z[:, :].rearrange("p (a b) -> p a b", a=TT)
        PROD = hi_z[0:CH + 1, :].bitcast(F32)[:, 0:4 * C].rearrange("p (a b) -> p a b", a=2)
        T0 = sb("T0", [P, 2, TT, C])
        QS0 = sb("QS0", [P, NH, NTOK], F16)
        KS0 = sb("KS0", [P, NH, NTOK], F16)
        V0 = sb("V0", [P, TT, C])
        odd = sb("odd", [P, GS * 3 * NTOK if GS * 3 * NTOK > 18432 else 18432], F16)
        QS1 = odd[:, 0:6144].rearrange("p (a b) -> p a b", a=NH)
        KS1 = odd[:, 6144:12288].rearrange("p (a b) -> p a b", a=NH)
        QKL = odd[:, 12288:15360].rearrange("p (a b) -> p a b", a=3)
        V1 = odd[:, 15360:18432].bitcast(F32).rearrange("p (a b) -> p a b", a=TT)
        QS, KS, V = [QS0, QS1], [KS0, KS1], [V0, V1]
        Z2 = odd[:, 0:GS * 3 * NTOK].rearrange("p (b h j n) -> p b h j n", b=GS, h=2, j=3)
        Y2 = odd[:, 0:GS * 3 * NTOK].bitcast(F32).rearrange("p (b h n) -> p b h n", b=GS, h=2)
        T1 = sb("T1", [P, GS, TT, C])
        T1H = T1[:, :, :, :].rearrange("p b (h t) c -> p b h (t c)", h=2)
        work = sb("work", [P, 9216])
        PS = [work[:, 0:1024].rearrange("p (a b) -> p a b", a=2), work[:, 1024:3072].rearrange("p (a b) -> p a b", a=2)]
        PTS = [work[:, 3072:5120].rearrange("p (a b) -> p a b", a=RING),
               work[:, 5120:9216].rearrange("p (a b) -> p a b", a=RING)]
        H = work[:, 0:6144].rearrange("p (h m n) -> p h m n", h=2, m=MH)
        JUNK = work[:, 0:2048].rearrange("p (a b) -> p a b", a=4)
        OS = work[0:CH, 0:2048].rearrange("p (h c n) -> p h c n", h=2, c=2)
        OT = work[:, 2048:2048 + 2 * 4 * C].rearrange("p (h n) -> p h n", h=2)
        oT = sb("oT", [CH, 2, P])
        rowsum = sb("rowsum", [P, U2])
        nmax = sb("nmax", [P, U2])
        stats = sb("stats", [P, TT, 6])
        mv = sb("mv", [P, TT, 2])
        rstd = sb("rstd", [P, TT])
        fin = sb("fin", [P, CH])
        gm = sb("gm", [P, 16])
        scratch = odd[:, :].bitcast(F32)
        W3f = scratch[:, 0:1728].rearrange("p (a b) -> p a b", a=3)
        W1f = scratch[:, 1728:4032].rearrange("p (a b) -> p a b", a=3)
        W1c = scratch[:, 4032:6336].rearrange("p (a b) -> p a b", a=3)
        W2f = scratch[:, 6336:7488].rearrange("p (a b) -> p a b", a=MH)
        W2c = scratch[:, 7488:8640].rearrange("p (a b) -> p a b", a=MH)

        amax, wscale, vback = sc[:, 0:3], sc[:, 3:6], sc[:, 6:7]
        qkback, qkprod = sc[:, 7:8], sc[:, 8:9]
        sum1, sum2 = sc[:, 10:15], sc[:, 15:20]
        run1, run2, gam1, gam2 = sc[:, 20:21], sc[:, 21:22], sc[:, 22:23], sc[:, 23:24]
        ge, gr, r1, c1 = sc[:, 24:25], sc[:, 25:26], sc[:, 26:27], sc[:, 27:28]
        ge2, gr2, r2, c2, c2n = sc[:, 28:29], sc[:, 29:30], sc[:, 30:31], sc[:, 31:32], sc[:, 32:33]
        clip_hi, clip_lo, rb1 = sc[:, 33:39], sc[:, 39:45], sc[:, 45:51]
        rqt = sc[0:CH, 51:53]
        xmax, xsum = sc[0:CH, 53:55], sc[0:CH, 55:57]
        rsum3 = sc[:, 57:60]
        xrec = sc[0:CH, 60:62]
        half = sc[:, 62:63]

        S = ctx.enter_context(nc.psum_tensor("S", [P, 2, 1024], F32))
        PT = [ctx.enter_context(nc.psum_tensor(f"PT{i}", [P, 512], F32)) for i in range(2)]
        OUT = ctx.enter_context(nc.psum_tensor("OUT", [P, 512], F32))
        FR = ctx.enter_context(nc.psum_tensor("FR", [P, 512], F32))
        FB = [FR[:, :], S[:, 0, 512:1024]]
        Y = [S[:, i // 2, 512 * (i % 2):512 * (i % 2) + 512] for i in range(4)]
        ZP = [FR[:, :], OUT[:, :]]

        w_in = sem("w_in")
        bias_in = sem("bias_in")
        cst_made = sem("cst_made")
        prep = sem("prep")
        prep_all = sem("prep_all")
        w_ready = sem("w_ready")
        x_in = sem("x_in")
        front_full = sem("front_full")
        front_free = [sem(f"front_free{i}") for i in range(2)]
        norm2_made = sem("norm2_made")
        rnorm_made = sem("rnorm_made")
        xsoft = sem("xsoft")
        xexp_made = sem("xexp_made")
        ln_step = sem("ln_step")
        rstd_made = sem("rstd_made")
        zlo_made = sem("zlo_made")
        qkhi_made = sem("qkhi_made")
        qklo_made = sem("qklo_made")
        stacked = [sem(f"stacked{i}") for i in range(2)]
        scores_full = sem("scores_full")
        max_made = sem("max_made")
        exp_made = sem("exp_made")
        pt_full = [sem(f"pt_full{i}") for i in range(2)]
        pt_free = [sem(f"pt_free{i}") for i in range(2)]
        pv_made = sem("pv_made")
        oT_made = sem("oT_made")
        t1_step = sem("t1_step")
        ln2_step = sem("ln2_step")
        rstd2_made = sem("rstd2_made")
        z2lo_made = sem("z2lo_made")
        z2t_full = sem("z2t_full")
        z2t_made = sem("z2t_made")
        y1_full = sem("y1_full")
        abs_made = sem("abs_made")
        max1_step = sem("max1_step")
        gam1_made = sem("gam1_made")
        quant1_step = sem("quant1_step")
        y_full = sem("y_full")
        clip_made = sem("clip_made")
        gelu_made = sem("gelu_made")
        y2_full = sem("y2_full")
        y2_made = sem("y2_made")
        max2_step = sem("max2_step")
        gam2_made = sem("gam2_made")
        quant2_step = sem("quant2_step")
        o_step = sem("o_step")
        ot_full = sem("ot_full")
        os_made = sem("os_made")
        stored = sem("stored")
        passed = sem("passed")

        def groups(e, body, tail):
            with e.Fori(0, NGROUPS) as g:
                with e.Fori(0, GS // 2) as p:
                    body(e.snap(g * (GS // 2) + p), p)
                tail(g)

        LAST = NGROUPS * GS // 2

        def after(pair, u, per, n):
            return pair * (2 * per) + (u * per + n)

        def wait_freed(e, pair, u, step, less=0):
            b = bank_of(step)
            e.wait_ge(front_free[b], after(pair, u, FRONT_FREES[b], freed(step) - less))

        def of_pair(pair, per, n):
            return pair * per + n

        def fronts_at(slot, run, parts, fronts):
            for u in range(fronts):
                for name, at in parts:
                    if UNITS * u + int(at) == slot:
                        run(name, u)

        def by_act(i, chunk):
            return chunk[1] == "p" and chunk[3] > 0

        def pt_copy(eng, copy, pair, i):
            _, _, m, c0, k = CHUNKS[i]
            eng.wait_ge(pt_full[i % 2], of_pair(pair, PT_PER, i // 2 + 1))
            if m >= 2 * RING:
                eng.wait_ge(pv_made, of_pair(pair, K2, triple_of(m - 2 * RING) + 1))
            copy(PTS[m % 2][:, m // 2 % RING, P * c0:P * (c0 + k)], PT[i % 2][:, 0:P * k]).then_inc(pt_free[i % 2], 1)

        def chunks_at(slot):
            return [(i, c) for i, c in enumerate(CHUNKS) if c[0] == slot]

        def alone(e):
            e.sem_inc(passed, 1)

        block = ctx.enter_context(nc.Block())

        @block.sync
        def _(sp):
            for dst, src in ((WT[0:CH + 1, 0, :], wa), (WT[0:CH, 1, :], wb), (WV[:, :, :], wv), (WPT[:, :, :], wpt),
                             (tempc[:, :], temp), (W3f[:, :, :], w3), (W1f[:, :, :], w1), (B1[:, :], b1),
                             (W2f[:, :, :], w2), (B2[:, :], b2)):
                sp.dma_start(dst, src).then_inc(w_in, 16)
            sp.wait_ge(cst_made, 11)
            sp.dma_start(IADD[CH:CH + 1, 0, :], bp).then_inc(bias_in, 16)

            def load_x(b):
                sp.dma_start(X[0:CH, :, :], x[b].rearrange("(c p) n -> p c n", p=CH)).then_inc(x_in, 16)

            def front(pair, u, more):
                if more:
                    sp.wait_ge(front_full, after(pair, u, FRONT_STEPS, STEPS.index("t3") + 1))
                    load_x(pair * 2 + (u + 1))
                sp.wait_ge(qklo_made, after(pair, u, 6, 6))
                for grp in range(2):
                    for r, stack, srcs in ((grp, QS, (QKH, QKL, QKH, QKL)), (2 + grp, KS, (QKH, QKH, QKL, QKL))):
                        for part in range(4):
                            sp.dma_start(stack[u % 2][32 * part:32 * part + 32, 3 * grp:3 * grp + 3, :],
                                         srcs[part][32 * r:32 * r + 32, :, :]).then_inc(stacked[grp], 16)

            def store(b, hf, n):
                sp.wait_ge(os_made, n)
                sp.dma_start(out[b].rearrange("(c p) n -> p c n", p=CH)[:, :, 512 * hf:512 * hf + 512],
                             OS[:, hf, :, :]).then_inc(stored, 16)

            sp.sem_inc(stored, 16)
            load_x(0)
            front(0, 0, True)

            def pair_body(pair, p):
                for u in range(2):
                    front(pair, u + 1, True)

            def group_tail(g):
                with sp.Fori(0, GS) as b:
                    for hf in range(2):
                        store(g * GS + b, hf, g * (2 * GS) + b * 2 + (hf + 1))

            groups(sp, pair_body, group_tail)
            front(LAST, 1, False)
            for u in range(2):
                for hf in range(2):
                    store(2 * LAST + u, hf, 4 * LAST + 2 * u + hf + 1)
            sp.wait_ge(stored, 16 * (2 * B + 1))

        @block.gpsimd
        def _(pool):
            pool.memset(ident[:, :], 0.0).then_inc(cst_made, 1)
            pool.memset(causal[:, :], 0.0).then_inc(cst_made, 1)
            pool.memset(IADD[:, :, :], 0.0).then_inc(cst_made, 1)
            pool.memset(blockmask[:, :, :], 0.0).then_inc(cst_made, 1)
            pool.memset(ones[:, :], 1.0).then_inc(cst_made, 1)
            pool.memset(halfneg[:, :], -0.5).then_inc(cst_made, 1)
            pool.memset(epst[:, :], LN_EPS).then_inc(cst_made, 1)
            pool.wait_ge(cst_made, 7)
            pool.affine_select(out=ident[:, :], in_=ident[:, :], compare_op=ALU.not_equal, fill=1.0, base=0,
                               pattern=[[-1, P]], channel_multiplier=1).then_inc(cst_made, 1)
            pool.affine_select(out=causal[:, :], in_=causal[:, :], compare_op=ALU.is_ge, fill=MASKED, base=0,
                               pattern=[[-1, P]], channel_multiplier=1).then_inc(cst_made, 1)
            pool.affine_select(out=IADD[0:CH, :, :], in_=IADD[0:CH, :, :], compare_op=ALU.not_equal, fill=1.0,
                               base=0, pattern=[[CH, 2], [-1, C]], channel_multiplier=1).then_inc(cst_made, 1)
            bm = blockmask[:, :, :].rearrange("p m (h d) -> p m h d", d=XD)
            pool.affine_select(out=bm, in_=bm, compare_op=ALU.is_ge, fill=MASKED, base=0,
                               pattern=[[0, 2], [-XD, CH // XD], [0, XD]], channel_multiplier=1).then_inc(cst_made, 1)
            pool.wait_ge(cst_made, 11)
            pool.affine_select(out=bm, in_=bm, compare_op=ALU.is_ge, fill=MASKED, base=XD - 1,
                               pattern=[[0, 2], [XD, CH // XD], [0, XD]], channel_multiplier=-1).then_inc(cst_made, 1)
            pool.tensor_copy(ident16[:, :], ident[:, :]).then_inc(cst_made, 1)
            pool.tensor_copy(identb[:, :], ident[:, :]).then_inc(cst_made, 1)
            pool.wait_ge(prep, 3)
            pool.partition_all_reduce(amax, sc[:, 33:36], P, RMAX).then_inc(prep_all, 1)
            pool.wait_ge(prep, 3 + 2 * NGROUPS)
            pool.partition_all_reduce(sc[:, 10:20], sc[:, 36:46], P, RADD).then_inc(prep_all, 1)
            pool.wait_ge(prep, 3 + 2 * NGROUPS + 3)
            pool.tensor_tensor(qkback, qkprod, half, ALU.pow).then_inc(prep_all, 1)

            def front(pair, u):
                pool.wait_ge(norm2_made, after(pair, u, 1, 1))
                pool.tensor_tensor(NK[:, :], NK[:, :], halfneg[0:CH, 0:4], ALU.pow).then_inc(rnorm_made, 1)
                pool.wait_ge(ln_step, after(pair, u, 25, 16))
                pool.tensor_tensor(rstd[:, :], mv[:, :, 1], epst[:, :], ALU.add).then_inc(rstd_made, 1)
                pool.wait_ge(rstd_made, after(pair, u, 2, 1))
                pool.tensor_tensor(rstd[:, :], rstd[:, :], halfneg[:, 0:TT], ALU.pow).then_inc(rstd_made, 1)
                pool.wait_ge(ln_step, after(pair, u, 25, 25))
                pool.tensor_tensor(zcat[:, :, C:2 * C], Z, zcat[:, :, 0:C], ALU.subtract).then_inc(zlo_made, 1)

            front(0, 0)

            def pair_body(pair, p):
                for u in range(2):
                    front(pair, u + 1)

            def group_tail(g):
                with pool.Fori(0, GS) as b:
                    ab = pool.snap(g * GS + b)
                    pool.wait_ge(ln2_step, ab * 25 + 16)
                    pool.tensor_tensor(rstd[:, :], mv[:, :, 1], epst[:, :], ALU.add).then_inc(rstd2_made, 1)
                    pool.wait_ge(rstd2_made, ab * 2 + 1)
                    pool.tensor_tensor(rstd[:, :], rstd[:, :], halfneg[:, 0:TT], ALU.pow).then_inc(rstd2_made, 1)
                    pool.wait_ge(ln2_step, ab * 25 + 25)
                    pool.tensor_tensor(zcat[:, :, C:2 * C], Z, zcat[:, :, 0:C], ALU.subtract).then_inc(z2lo_made, 1)
                pool.wait_ge(max1_step, (g + 1) * (GS * 14 + 1))
                alone(pool)
                pool.partition_all_reduce(gam1, run1, P, RMAX).then_inc(gam1_made, 1)
                pool.wait_ge(max2_step, (g + 1) * (GS * 2 + 1))
                alone(pool)
                pool.partition_all_reduce(gam2, run2, P, RMAX).then_inc(gam2_made, 1)

            groups(pool, pair_body, group_tail)
            front(LAST, 1)

        @block.tensor
        def _(pe):
            mm = nc.tensor.matmul
            tr = nc.tensor.transpose
            pe.wait_ge(cst_made, 14)
            pe.wait_ge(w_in, 16 * 10)
            pe.wait_ge(w_ready, 1)

            def front_part(name, pair, u):
                FR = FB[bank_of({"g0a": "g0", "g1a": "g1"}.get(name, name))]
                if name not in ("g0", "g1"):
                    step = {"g0a": "g0", "g1a": "g1"}.get(name, name)
                    i = STEPS.index(step)
                    if i >= 2:
                        wait_freed(pe, pair, u, STEPS[i - 2])
                    elif u or not isinstance(pair, int):
                        wait_freed(pe, pair, u - 1, STEPS[i - 2])
                    if step in NEEDS:
                        wait_freed(pe, pair, u, NEEDS[step])
                if name.startswith("xt"):
                    k = int(name[2:])
                    if k == 0:
                        pe.wait_ge(x_in, after(pair, u, 16, 16))
                    for t in range(2):
                        cols = slice((2 * k + t) * P, (2 * k + t + 1) * P)
                        o = t * (C + 1)
                        tr(FR[:, o:o + CH + 1], X[0:CH + 1, 0, cols], ident[0:CH + 1, 0:CH + 1])
                        last = tr(FR[:, o + CH + 1:o + C + 1], X[0:CH, 1, cols], ident[0:CH, 0:CH])
                elif name in ("g0a", "g0", "g1a", "g1"):
                    c0, m = (0, CH + 1) if name[1] == "0" else (CH + 1, CH)
                    o = 0
                    for t in (range(0, 4) if name.endswith("a") else range(4, 8)):
                        last = mm(FR[0:m, o:o + C + 1], XT[:, t, c0:c0 + m], XT[:, t, :],
                                  start=(t == 0), stop=(t == TT - 1))
                    if name.endswith("a"):
                        return
                elif name in ("wg0", "wg1"):
                    c0, m = (0, CH + 1) if name == "wg0" else (CH + 1, CH)
                    mm(FR[0:m, 0:2 * C], G[0:CH + 1, 0, c0:c0 + m], WT[0:CH + 1, 0, :], start=True, stop=False)
                    last = mm(FR[0:m, 0:2 * C], G[0:CH, 1, c0:c0 + m], WT[0:CH, 1, :], start=False, stop=True)
                elif name == "na":
                    for j in range(4):
                        for c, m in ((0, CH + 1), (1, CH)):
                            mm(FR[0:CH, C + j:C + j + 1], PROD[0:m, c, CH * j:CH * j + CH], ones[0:m, 0:1],
                               start=(c == 0), stop=(c == 1))
                    for j in range(2):
                        for c, m in ((0, CH + 1), (1, CH)):
                            last = mm(FR[0:CH, 256 + CH * j:256 + CH * j + CH], WT[0:m, c, CH * j:CH * j + CH],
                                      TK[0:m, c, CH * j:CH * j + CH], start=(c == 0), stop=(c == 1))
                elif name == "rb":
                    pe.wait_ge(xsoft, after(pair, u, XSOFT, 2))
                    last = mm(FR[0:CH, 0:C], ones[0:CH, :], RD[:, :, :].rearrange("p a b -> p (a b)"),
                              start=True, stop=True)
                elif name == "u":
                    pe.wait_ge(xsoft, after(pair, u, XSOFT, XSOFT))
                    for j in range(2):
                        last = mm(FR[0:CH, C * j:C * j + C], ATT[:, j, :], WPT[:, j, :], start=True, stop=True)
                elif name == "mt":
                    for c, c0, m in ((0, 0, CH + 1), (1, CH + 1, CH)):
                        for j in range(2):
                            last = mm(FR[0:m, C * c:C * c + C], WV[:, j, c0:c0 + m], U[:, j, :],
                                      start=(j == 0), stop=(j == 1))
                elif name[0] == "t":
                    k = int(name[1:])
                    for t in range(2):
                        cols = slice((2 * k + t) * P, (2 * k + t + 1) * P)
                        mm(FR[:, C * t:C * t + C], X[0:CH + 1, 0, cols], MT[0:CH + 1, 0, :], start=True, stop=False)
                        last = mm(FR[:, C * t:C * t + C], X[0:CH, 1, cols], MT[0:CH, 1, :], start=False, stop=True)
                elif name[0] == "z":
                    k = int(name[1:])
                    if k == 0:
                        pe.wait_ge(zlo_made, after(pair, u, 1, 1))
                    last = turn_z(FR, k)
                elif name.startswith("qk"):
                    i = int(name[2:])
                    m, hf = i // 2, i % 2
                    for j in range(3):
                        for w in (W3h, W3l):
                            last = mm(FR, w[:, j, P * m:P * m + P], zt[:, j, 512 * hf:512 * hf + 512],
                                      start=(j == 0 and w is W3h), stop=(j == 2 and w is W3l))
                else:
                    k = int(name[1:])
                    for t in range(2):
                        for j in range(3):
                            for w in (W3h, W3l):
                                last = mm(FR[:, C * t:C * t + C], zt[:, j, (2 * k + t) * P:(2 * k + t + 1) * P],
                                          w[:, j, 2 * C:3 * C], start=(j == 0 and w is W3h),
                                          stop=(j == 2 and w is W3l))
                last.then_inc(front_full, 1)

            def turn_z(bank, k):
                v = bank.bitcast(F16).rearrange("p (j n) -> p j n", j=4)
                for t in range(2):
                    for j in range(3):
                        last = tr(v[:, j, P * t:P * t + P], zcat[:, 2 * k + t, P * j:P * j + P], ident16[:, :])
                return last

            pe.sem_inc(ot_full, 1)
            for name in SLOTS:
                front_part(name, 0, 0)

            def attention(pair, fronts):
                for n in range(LAST_SLOT + 1):
                    if n < U2:
                        u, h, qt = n // UNITS, 3 * (n % UNITS // 24) + n % 6 // 2, qtile(n)
                        if n % 24 == 0:
                            pe.wait_ge(stacked[n % UNITS // 24], after(pair, u, STACKS, STACKS))
                        if n >= 2:
                            pe.wait_ge(exp_made, of_pair(pair, U2, n - 1))
                        q = QS[u][:, h, P * qt:P * qt + P]
                        w = P * (qt + 1)
                        for c0 in range(0, w, 512):
                            mm(S[:, n % 2, c0:min(w, c0 + 512)], q, KS[u][:, h, c0:min(w, c0 + 512)],
                               start=True, stop=c0 + 512 < w)
                        mm(S[:, n % 2, w - P:w], identb[:, :], causal[:, :], start=False,
                           stop=True).then_inc(scores_full, 1)
                    for i, (_, kind, m, c0, k) in chunks_at(n):
                        bank = PT[i % 2]
                        if kind == "p" and c0 == 0:
                            pe.wait_ge(exp_made, of_pair(pair, U2, m + 1))
                        if kind == "p":
                            if i >= 2:
                                pe.wait_ge(pt_free[i % 2], of_pair(pair, PT_PER, i // 2))
                            for j in range(c0, c0 + k):
                                last = tr(bank[:, P * (j - c0):P * (j - c0) + P], PS[m % 2][:, m // 2 % 2, P * j:P * j + P],
                                          ident[:, :])
                            last.then_inc(pt_full[i % 2], 1)
                    for k in triples_at(n, PV_AT):
                        u, grp, qt = k // (K2 // 2), k % (K2 // 2) // 8, qtile(unit_of(k, 0))
                        done = [i for i, c in enumerate(CHUNKS) if c[1] == "p" and c[2] <= unit_of(k, 2)]
                        for b in range(2):
                            pe.wait_ge(pt_free[b], of_pair(pair, PT_PER, max(i for i in done if i % 2 == b) // 2 + 1))
                        if k % (K2 // 2) == 0:
                            for step in STEPS[-2:]:
                                wait_freed(pe, pair, u, step)
                        if k:
                            pe.wait_ge(oT_made, of_pair(pair, K2, k))
                        for j in range(qt + 1):
                            for hh in range(3):
                                h = 3 * grp + hh
                                last = mm(OUT[32 * hh:32 * hh + 32, 0:P],
                                          V[u][:, j, D * h:D * h + D], PTS[k % 2][:, unit_of(k, hh) // 2 % RING, P * j:P * j + P],
                                          start=(j == 0), stop=(j == qt), tile_position=(0, 32 * hh))
                        last.then_inc(pv_made, 1)
                    for i, (_, kind, k, _, _) in chunks_at(n):
                        if kind == "o":
                            pe.wait_ge(pt_free[i % 2], of_pair(pair, PT_PER, i // 2))
                            pe.wait_ge(oT_made, of_pair(pair, K2, k + 1))
                            tr(PT[i % 2][:, 0:CH], oT[:, k % 2, :], ident[0:CH, 0:CH]).then_inc(pt_full[i % 2], 1)
                    fronts_at(n, lambda name, u: front_part(name, pair, u + 1), SLOTS.items(), fronts)

            def ffn1(rhs, bank, i):
                for j in range(3):
                    last = mm(bank, W1b[:, j, P * (i % 6):P * (i % 6) + P], rhs[:, j, :],
                              start=(j == 0), stop=(j == 2))
                return last

            def turn_out(src, hf):
                for c in range(2):
                    for t in range(4):
                        o = 512 * c + P * t
                        last = tr(S[0:CH, hf, o:o + P], src(t, c), ident[:, :])
                return last

            def pair_body(pair, p):
                attention(pair, 2)

            def group_tail(g):
                nb = g + 1
                pe.wait_ge(t1_step, nb * (GS * UNITS))
                for i in range(2):
                    pe.wait_ge(front_free[i], nb * (GS * FRONT_FREES[i]) + FRONT_FREES[i])
                for st in stacked:
                    pe.wait_ge(st, nb * (GS * STACKS) + STACKS)
                alone(pe)
                with pe.Fori(0, GS) as b:
                    ab = pe.snap(g * GS + b)
                    pe.wait_ge(z2lo_made, ab + 1)
                    for k in range(4):
                        if k >= 2:
                            pe.wait_ge(z2t_made, ab * 4 + (k - 1))
                        turn_z(ZP[k % 2], k).then_inc(z2t_full, 1)
                    for i in range(12):
                        if i % 6 == 0:
                            pe.wait_ge(z2t_made, ab * 4 + (2 + 2 * (i // 6)))
                        if i >= 4:
                            pe.wait_ge(abs_made, ab * 12 + (i - 3))
                        ffn1(Z2[:, b, i // 6], Y[i % 4], i).then_inc(y1_full, 1)
                pe.wait_ge(abs_made, nb * (GS * 12))
                alone(pe)
                with pe.Fori(0, GS) as b:
                    ab = pe.snap(g * GS + b)
                    for i in range(12):
                        if i >= 4:
                            pe.wait_ge(clip_made, ab * 12 + (i - 3))
                        ffn1(Z2[:, b, i // 6], Y[i % 4], i).then_inc(y_full, 1)
                    for tp in range(4):
                        hf = tp // 2
                        pe.wait_ge(gelu_made, ab * 12 + 6 * (hf + 1))
                        if tp >= 2:
                            pe.wait_ge(y2_made, ab * 4 + (tp - 1))
                        for t in range(2):
                            o = P * (2 * (tp % 2) + t)
                            for m in range(MH):
                                last = mm(PT[tp % 2][:, C * t:C * t + C], H[:, hf, m, o:o + P], W2b[:, m, :],
                                          start=(m == 0), stop=(m == MH - 1))
                        last.then_inc(y2_full, 1)
                with pe.Fori(0, GS) as b:
                    ab = pe.snap(g * GS + b)
                    for hf in range(2):
                        pe.wait_ge(o_step, ab * 4 + (2 * hf + 2))
                        if hf == 1:
                            pe.wait_ge(os_made, ab * 2 + 1)
                        turn_out(lambda t, c: OT[:, hf, C * t + CH * c:C * t + CH * c + CH], hf).then_inc(ot_full, 1)
                pe.wait_ge(os_made, nb * (2 * GS))

            groups(pe, pair_body, group_tail)
            attention(LAST, 1)
            pe.wait_ge(t1_step, UNITS * B)
            for u in range(2):
                for hf in range(2):
                    if u:
                        pe.wait_ge(os_made, 4 * LAST + hf + 1)
                    turn_out(lambda t, c: T1[:, u, 4 * hf + t, CH * c:CH * c + CH], hf).then_inc(ot_full, 1)

        @block.scalar
        def _(act):
            A = nc.scalar.activation
            act.wait_ge(w_ready, 1)

            def front_part(name, pair, u):
                f = u % 2
                FR = FB[bank_of(name)] if name in STEPS else None
                if name in ("g0a", "g1a", "na", "rb"):
                    return
                if name == "xexp":
                    act.wait_ge(xsoft, after(pair, u, XSOFT, 6))
                    for j in range(2):
                        A(ATT[:, j, :], LOG[:, j, :], ACT.Exp, bias=xmax[:, j:j + 1],
                          accum_out=xsum[:, j:j + 1]).then_inc(xexp_made, 1)
                    return
                if name not in STEPS or name == "mt":
                    return
                act.wait_ge(front_full, after(pair, u, FRONT_STEPS, STEPS.index(name) + 1))
                if name.startswith("xt"):
                    k = int(name[2:])
                    o = A(XT[:, 2 * k:2 * k + 2, :], FR[:, 0:2 * (C + 1)].rearrange("p (t c) -> p t c", t=2), ACT.Copy)
                elif name in ("g0", "g1"):
                    c, m = int(name[1]), CH + 1 - int(name[1])
                    o = A(G[0:m, c, :], FR[0:m, 0:C + 1], ACT.Copy)
                elif name in ("wg0", "wg1"):
                    c, m = int(name[2]), CH + 1 - int(name[2])
                    wait_freed(act, pair, u, name, 1)
                    o = A(TK[0:m, c, :], FR[0:m, C:2 * C], ACT.Copy)
                elif name == "u":
                    o = A(U[:, :, :], FR[0:CH, 0:2 * C].rearrange("p (a b) -> p a b", a=2), ACT.Copy)
                elif name[0] == "t":
                    k = int(name[1:])
                    o = A(T0[:, f, 2 * k:2 * k + 2, :], FR[:, 0:2 * C].rearrange("p (a b) -> p a b", a=2), ACT.Copy)
                elif name[0] == "z":
                    k = int(name[1:])
                    v = FR.bitcast(F16).rearrange("p (j n) -> p j n", j=4)
                    o = A(zt[:, :, 256 * k:256 * k + 256], v[:, 0:3, :], ACT.Copy)
                elif name.startswith("qk"):
                    i = int(name[2:])
                    A(QKH[:, i // 2, 512 * (i % 2):512 * (i % 2) + 512], FR, ACT.Copy,
                      scale=qkback).then_inc(qkhi_made, 1)
                    return
                else:
                    k = int(name[1:])
                    o = A(V[f][:, 2 * k:2 * k + 2, :], FR[:, 0:2 * C].rearrange("p (a b) -> p a b", a=2), ACT.Copy,
                          scale=vback)
                o.then_inc(front_free[bank_of(name)], 1)

            order = list(SLOTS.items()) + [("xexp", SMALL_SLOTS["xexp"])]
            order.sort(key=lambda a: a[1])
            for name, _ in order:
                front_part(name, 0, 0)

            def attention(pair, fronts):
                for n in range(LAST_SLOT + 1):
                    for k in triples_at(n, OT_AT):
                        act.wait_ge(pv_made, of_pair(pair, K2, k + 1))
                        if k >= 2:
                            act.wait_ge(t1_step, of_pair(pair, 3 * K2, 3 * (k - 2) + 2))
                        A(oT[:, k % 2, :], OUT[0:CH, 0:P], ACT.Copy).then_inc(oT_made, 1)
                    if n < U2:
                        act.wait_ge(max_made, of_pair(pair, U2, n + 1))
                        if n >= 4:
                            i = max(i for i, c in enumerate(CHUNKS) if c[1] == "p" and c[2] == n - 4)
                            act.wait_ge(pt_full[i % 2], of_pair(pair, PT_PER, i // 2 + 1))
                        w = P * (qtile(n) + 1)
                        A(PS[n % 2][:, n // 2 % 2, 0:w], S[:, n % 2, 0:w], ACT.Exp, bias=nmax[:, n:n + 1],
                          accum_out=rowsum[:, n:n + 1]).then_inc(exp_made, 1)
                    for i, c in chunks_at(n):
                        if by_act(i, c):
                            pt_copy(act, lambda o, x: A(o, x, ACT.Copy), pair, i)
                    fronts_at(n, lambda name, u: front_part(name, pair, u + 1), order, fronts)

            def put_out(hf, full):
                act.wait_ge(ot_full, full)
                A(OS[:, hf, :, :], S[0:CH, hf, :].rearrange("p (c n) -> p c n", c=2), ACT.Copy).then_inc(os_made, 1)

            def pair_body(pair, p):
                attention(pair, 2)

            def group_tail(g):
                with act.Fori(0, GS) as b:
                    ab = act.snap(g * GS + b)
                    for i in range(12):
                        act.wait_ge(y1_full, ab * 12 + (i + 1))
                        if i >= 4:
                            act.wait_ge(max1_step, ab * 14 + g + (i - 3 + 1))
                        A(JUNK[:, i % 4, :], Y[i % 4], ACT.Abs, bias=B1[:, i % 6:i % 6 + 1]).then_inc(abs_made, 1)
                act.wait_ge(quant1_step, (g + 1) * 7)
                with act.Fori(0, GS) as b:
                    ab = act.snap(g * GS + b)
                    for i in range(12):
                        act.wait_ge(clip_made, ab * 12 + (i + 1))
                        h = H[:, i // 6, i % 6, :]
                        A(h, h, ACT.Gelu, bias=rb1[:, i % 6:i % 6 + 1], scale=r1).then_inc(gelu_made, 1)
                with act.Fori(0, GS) as b:
                    ab = act.snap(g * GS + b)
                    for hf in range(2):
                        if hf == 0:
                            act.wait_ge(stored, ab * 32 + 16)
                        put_out(hf, ab * 2 + (hf + 2))
                act.wait_ge(stored, (g + 1) * (GS * 32) + 16)

            groups(act, pair_body, group_tail)
            attention(LAST, 1)
            for u in range(2):
                act.wait_ge(stored, 16 * (4 * LAST + 2 * u + 1))
                for hf in range(2):
                    put_out(hf, 4 * LAST + 2 * u + hf + 2)

        @block.vector
        def _(dve):
            v = nc.vector
            dve.wait_ge(w_in, 16 * 10)
            qk = W3f[:, :, 0:2 * C].rearrange("p j (m s d) -> p j m s d", m=3, s=2)
            kinds = (qk[:, :, :, 0, :], qk[:, :, :, 1, :], W3f[:, :, 2 * C:3 * C])
            for i, w in enumerate(kinds):
                v.tensor_reduce(sc[:, 33 + i:34 + i], w, AX.XY if i == 2 else AX.XYZ, ALU.max,
                                apply_absolute_value=True).then_inc(prep, 1)
            g1 = HID // NGROUPS
            g2 = C // NGROUPS
            for g in range(NGROUPS):
                v.tensor_reduce(sc[:, 36 + g:37 + g], W1f[:, :, g1 * g:g1 * g + g1], AX.XY, ALU.add).then_inc(prep, 1)
            for g in range(NGROUPS):
                v.tensor_reduce(sc[:, 41 + g:42 + g], W2f[:, :, g2 * g:g2 * g + g2], AX.XY, ALU.add).then_inc(prep, 1)
            chain = [3 + 2 * NGROUPS]

            def link(ins):
                chain[0] += 1
                ins.then_inc(prep, 1)
                dve.wait_ge(prep, chain[0])

            dve.wait_ge(prep_all, 1)
            v.memset(half, 0.5).then_inc(prep, 1)
            chain[0] += 1
            v.tensor_scalar(amax, amax, 1e-18, None, ALU.max).then_inc(prep, 1)
            chain[0] += 1
            dve.wait_ge(prep, chain[0])
            link(v.tensor_scalar(qkprod, amax[:, 0:1], amax[:, 1:2], 1.0 / (WTOP * WTOP * float(np.sqrt(C))),
                                 ALU.mult, ALU.mult))
            link(v.reciprocal(wscale, amax))
            link(v.tensor_scalar(wscale, wscale, WTOP, None, ALU.mult))
            link(v.tensor_scalar(vback, amax[:, 2:3], 1.0 / WTOP, None, ALU.mult))
            for i, w in enumerate(kinds):
                link(v.tensor_scalar(w, w, wscale[:, i:i + 1], None, ALU.mult))
            link(v.tensor_copy(W3h[:, :, :], W3f[:, :, :]))
            link(v.tensor_tensor(W3l[:, :, :], W3f[:, :, :], W3h[:, :, :], ALU.subtract))
            dve.wait_ge(prep_all, 2)
            link(v.tensor_scalar(sum1, sum1, 1.0 / (2 * g1 * C), None, ALU.mult))
            link(v.tensor_scalar(sum2, sum2, 1.0 / (g2 * HID), None, ALU.mult))
            link(v.memset(W1b[:, :, :], 0.0))
            link(v.memset(W2b[:, :, :], 0.0))
            for wf, wc, wbin, gs, means in ((W1f, W1c, W1b, g1, sum1), (W2f, W2c, W2b, g2, sum2)):
                for g in range(NGROUPS):
                    cols = slice(gs * g, gs * g + gs)
                    link(v.tensor_scalar(wc[:, :, cols], wf[:, :, cols], means[:, g:g + 1], None, ALU.is_lt))
                    link(v.scalar_tensor_tensor(out=wbin[:, :, cols], in0=wf[:, :, cols], scalar=means[:, g:g + 1],
                                                in1=wc[:, :, cols], op0=ALU.is_gt, op1=ALU.subtract))
            dve.wait_ge(prep_all, 3)
            dve.wait_ge(cst_made, 14)
            dve.wait_ge(bias_in, 16)
            v.memset(X[CH:CH + 1, 0, :], 1.0).then_inc(w_ready, 1)

            def layer_norm(src, step, step_base, rs_sem, rs_value, part):
                if part == "stats":
                    for t in range(TT):
                        v.bn_stats(stats[:, t, :], src(t)).then_inc(step, 1)
                    for t in range(TT):
                        dve.wait_ge(step, step_base + (t + 1))
                        alone(dve)
                        v.bn_aggr(mv[:, t, :], stats[:, t, :]).then_inc(step, 1)
                else:
                    dve.wait_ge(rs_sem, rs_value)
                    for t in range(TT):
                        v.tensor_scalar(Z[:, t, :], src(t), mv[:, t, 0:1], rstd[:, t:t + 1], ALU.subtract,
                                        ALU.mult).then_inc(step, 1)
                    dve.wait_ge(step, step_base + 24)
                    v.tensor_copy(zcat[:, :, 0:C], Z).then_inc(step, 1)

            def front_part(name, pair, u):
                f = u % 2
                step = {"norms": "na", "logits": "rb"}.get(name, name)
                FR, free = (FB[bank_of(step)], front_free[bank_of(step)]) if step in STEPS else (None, None)
                if name in ("wg0", "wg1"):
                    c, m = int(name[2]), CH + 1 - int(name[2])
                    if name == "wg0" and u:
                        for st in stacked:
                            dve.wait_ge(st, after(pair, u, STACKS, 0))
                    dve.wait_ge(front_full, after(pair, u, FRONT_STEPS, STEPS.index(name) + 1))
                    v.tensor_tensor(PROD[0:m, c, :], FR[0:m, 0:2 * C], WT[0:m, c, :], ALU.mult).then_inc(free, 1)
                elif name == "norms":
                    dve.wait_ge(front_full, after(pair, u, FRONT_STEPS, STEPS.index("na") + 1))
                    v.tensor_scalar(NK[:, :], FR[0:CH, C:C + 4], NORM_EPS2, None, ALU.max).then_inc(norm2_made, 1)
                    v.tensor_copy(LOG, FR[0:CH, 256:256 + C].rearrange("p (a b) -> p a b", a=2)).then_inc(free, 1)
                elif name == "rdiag":
                    dve.wait_ge(rnorm_made, after(pair, u, 1, 1))
                    v.tensor_tensor(RD[:, :, :], ident[0:CH, 0:CH].unsqueeze(1).broadcast_to([CH, 2, CH]),
                                    NK[:, 2:4].unsqueeze(2).broadcast_to([CH, 2, CH]), ALU.mult).then_inc(xsoft, 1)
                    v.tensor_tensor(rqt, NK[:, 0:2], tempc[:, :], ALU.mult).then_inc(xsoft, 1)
                elif name == "logits":
                    dve.wait_ge(front_full, after(pair, u, FRONT_STEPS, STEPS.index("rb") + 1))
                    dve.wait_ge(xsoft, after(pair, u, XSOFT, 2))
                    for j in range(2):
                        v.scalar_tensor_tensor(out=LOG[:, j, :], in0=LOG[:, j, :], scalar=rqt[:, j:j + 1],
                                               in1=FR[0:CH, CH * j:CH * j + CH],
                                               op0=ALU.mult, op1=ALU.mult).then_inc(xsoft, 1)
                    dve.wait_ge(xsoft, after(pair, u, XSOFT, 4))
                    v.tensor_tensor(LOG, LOG, blockmask[:, :, :], ALU.add).then_inc(xsoft, 1)
                    dve.wait_ge(xsoft, after(pair, u, XSOFT, 5))
                    dve.sem_inc(free, 1)
                    v.tensor_reduce(xmax, LOG, AX.X, ALU.max, negate=True).then_inc(xsoft, 1)
                elif name == "attn":
                    dve.wait_ge(xexp_made, after(pair, u, 2, 2))
                    v.reciprocal(xrec, xsum).then_inc(xsoft, 1)
                    dve.wait_ge(xsoft, after(pair, u, XSOFT, 7))
                    for j in range(2):
                        v.tensor_scalar(ATT[:, j, :], ATT[:, j, :], xrec[:, j:j + 1], None,
                                        ALU.mult).then_inc(xsoft, 1)
                elif name == "mt":
                    dve.wait_ge(front_full, after(pair, u, FRONT_STEPS, STEPS.index("mt") + 1))
                    for c in range(2):
                        m = CH + 1 - c
                        v.tensor_tensor(MT[0:m, c, :], FR[0:m, C * c:C * c + C], IADD[0:m, c, :],
                                        ALU.add).then_inc(free, 1)
                elif name in ("ln_stats", "ln_norm"):
                    if name == "ln_stats":
                        wait_freed(dve, pair, u, "t2")
                        wait_freed(dve, pair, u, "t3")
                    layer_norm(lambda t: T0[:, f, t, :], ln_step, after(pair, u, 25, 0), rstd_made,
                               after(pair, u, 2, 2), name[3:])
                elif name.startswith("qk"):
                    i = int(name[2:])
                    dve.wait_ge(qkhi_made, after(pair, u, 6, i + 1))
                    cols = slice(512 * (i % 2), 512 * (i % 2) + 512)
                    v.scalar_tensor_tensor(out=QKL[:, i // 2, cols], in0=FR, scalar=qkback,
                                           in1=QKH[:, i // 2, cols], op0=ALU.mult,
                                           op1=ALU.subtract).then_inc(qklo_made, 1)
                    dve.wait_ge(qklo_made, after(pair, u, 6, i + 1))
                    dve.sem_inc(free, 1)

            order = list(SLOTS.items()) + [a for a in SMALL_SLOTS.items() if a[0] != "xexp"]
            order.sort(key=lambda a: a[1])
            for name, _ in order:
                front_part(name, 0, 0)

            def attention(pair, fronts, slot):
                for n in range(LAST_SLOT + 1):
                    if n < U2:
                        dve.wait_ge(scores_full, of_pair(pair, U2, n + 1))
                        v.tensor_reduce(nmax[:, n:n + 1], S[:, n % 2, 0:P * (qtile(n) + 1)], AX.X, ALU.max,
                                        negate=True).then_inc(max_made, 1)
                    for i, c in chunks_at(n):
                        if c[1] == "p" and not by_act(i, c):
                            pt_copy(dve, v.tensor_copy, pair, i)
                        if c[1] == "o":
                            k = c[2]
                            base = of_pair(pair, 3 * K2, 3 * k)
                            dve.wait_ge(pt_full[i % 2], of_pair(pair, PT_PER, i // 2 + 1))
                            v.reciprocal(rsum3, rowsum[:, unit_of(k, 0):unit_of(k, 2) + 1:2]).then_inc(t1_step, 1)
                            dve.wait_ge(t1_step, base + 1)
                            v.tensor_tensor(fin[:, :].rearrange("p (h d) -> p h d", h=3),
                                            PT[i % 2][:, 0:CH].rearrange("p (h d) -> p h d", h=3),
                                            rsum3[:, 0:3].unsqueeze(2).broadcast_to([P, 3, D]),
                                            ALU.mult).then_inc(t1_step, 1)
                            dve.wait_ge(t1_step, base + 2)
                            dve.sem_inc(pt_free[i % 2], 1)
                            u, qt, grp = k // (K2 // 2), qtile(unit_of(k, 0)), k % (K2 // 2) // 8
                            cols = slice(CH * grp, CH * grp + CH)
                            v.tensor_tensor(T1[:, slot + u, qt, cols], fin[:, :], T0[:, u, qt, cols],
                                            ALU.add).then_inc(t1_step, 1)
                    fronts_at(n, lambda name, u: front_part(name, pair, u + 1), order, fronts)

            def pair_body(pair, p):
                attention(pair, 2, p * 2)

            def group_tail(g):
                nb = g + 1
                for st in stacked:
                    dve.wait_ge(st, nb * (GS * STACKS) + STACKS)
                v.memset(run1, 0.0).then_inc(max1_step, 1)
                with dve.Fori(0, GS) as b:
                    ab = dve.snap(g * GS + b)
                    for part in ("stats", "norm"):
                        layer_norm(lambda t: T1[:, b, t, :], ln2_step, ab * 25, rstd2_made, ab * 2 + 2, part)
                    for k in range(4):
                        dve.wait_ge(z2t_full, ab * 4 + (k + 1))
                        zv = ZP[k % 2].bitcast(F16).rearrange("p (j n) -> p j n", j=4)
                        v.tensor_scalar(Z2[:, b, k // 2, :, 256 * (k % 2):256 * (k % 2) + 256], zv[:, 0:3, :], 1.0,
                                        None, ALU.mult).then_inc(z2t_made, 1)
                    base = ab * 14 + (g + 1)
                    for i in range(12):
                        dve.wait_ge(abs_made, ab * 12 + (i + 1))
                        v.tensor_reduce(gm[:, i:i + 1], JUNK[:, i % 4, :], AX.X, ALU.max).then_inc(max1_step, 1)
                    dve.wait_ge(max1_step, base + 12)
                    v.tensor_reduce(gm[:, 12:13], gm[:, 0:12], AX.X, ALU.max).then_inc(max1_step, 1)
                    dve.wait_ge(max1_step, base + 13)
                    v.tensor_tensor(run1, run1, gm[:, 12:13], ALU.max).then_inc(max1_step, 1)
                dve.wait_ge(gam1_made, nb)
                q0 = g * 7
                v.tensor_scalar(ge, gam1, Q_EPS, None, ALU.add).then_inc(quant1_step, 1)
                dve.wait_ge(quant1_step, q0 + 1)
                v.reciprocal(gr, ge).then_inc(quant1_step, 1)
                v.tensor_scalar(c1, ge, (QB - Q_EPS) / QB, None, ALU.mult).then_inc(quant1_step, 1)
                dve.wait_ge(quant1_step, q0 + 2)
                v.tensor_scalar(r1, gr, QB, None, ALU.mult).then_inc(quant1_step, 1)
                dve.wait_ge(quant1_step, q0 + 4)
                v.tensor_scalar(clip_hi, B1[:, :], -1.0, c1, ALU.mult, ALU.add).then_inc(quant1_step, 1)
                v.tensor_scalar(clip_lo, B1[:, :], -1.0, c1, ALU.mult, ALU.subtract).then_inc(quant1_step, 1)
                v.tensor_scalar(rb1, B1[:, :], r1, None, ALU.mult).then_inc(quant1_step, 1)
                dve.wait_ge(quant1_step, q0 + 7)
                v.memset(run2, 0.0).then_inc(max2_step, 1)
                with dve.Fori(0, GS) as b:
                    ab = dve.snap(g * GS + b)
                    for i in range(12):
                        dve.wait_ge(y_full, ab * 12 + (i + 1))
                        v.tensor_scalar(H[:, i // 6, i % 6, :], Y[i % 4], clip_hi[:, i % 6:i % 6 + 1],
                                        clip_lo[:, i % 6:i % 6 + 1], ALU.min, ALU.max).then_inc(clip_made, 1)
                    for tp in range(4):
                        dve.wait_ge(y2_full, ab * 4 + (tp + 1))
                        o = 2 * C * (tp % 2)
                        v.tensor_tensor(Y2[:, b, tp // 2, o:o + 2 * C].rearrange("p (a c) -> p a c", a=2),
                                        PT[tp % 2][:, 0:2 * C].rearrange("p (a c) -> p a c", a=2),
                                        B2[:, :].unsqueeze(1).broadcast_to([P, 2, C]), ALU.add).then_inc(y2_made, 1)
                    base = ab * 2 + (g + 1)
                    dve.wait_ge(y2_made, ab * 4 + 4)
                    alone(dve)
                    v.tensor_reduce(gm[:, 13:14], Y2[:, b], AX.XY, ALU.max,
                                    apply_absolute_value=True).then_inc(max2_step, 1)
                    dve.wait_ge(max2_step, base + 1)
                    v.tensor_tensor(run2, run2, gm[:, 13:14], ALU.max).then_inc(max2_step, 1)
                dve.wait_ge(gam2_made, nb)
                q0 = g * 5
                v.tensor_scalar(ge2, gam2, Q_EPS, None, ALU.add).then_inc(quant2_step, 1)
                dve.wait_ge(quant2_step, q0 + 1)
                v.reciprocal(gr2, ge2).then_inc(quant2_step, 1)
                v.tensor_scalar(c2, ge2, (QB - Q_EPS) / QB, None, ALU.mult).then_inc(quant2_step, 1)
                v.tensor_scalar(c2n, ge2, -(QB - Q_EPS) / QB, None, ALU.mult).then_inc(quant2_step, 1)
                dve.wait_ge(quant2_step, q0 + 4)
                v.tensor_scalar(r2, gr2, QB, None, ALU.mult).then_inc(quant2_step, 1)
                dve.wait_ge(quant2_step, q0 + 5)
                alone(dve)
                with dve.Fori(0, GS) as b:
                    ab = dve.snap(g * GS + b)
                    for hf in range(2):
                        dve.wait_ge(ot_full, ab * 2 + 1)
                        v.tensor_scalar(OT[:, hf, :], Y2[:, b, hf, :], c2, c2n, ALU.min, ALU.max).then_inc(o_step, 1)
                        dve.wait_ge(o_step, ab * 4 + (2 * hf + 1))
                        v.scalar_tensor_tensor(out=OT[:, hf, :], in0=OT[:, hf, :], scalar=r2, in1=T1H[:, b, hf, :],
                                               op0=ALU.mult, op1=ALU.add).then_inc(o_step, 1)

            groups(dve, pair_body, group_tail)
            attention(LAST, 1, 0)


def kernel(x, L0_conv_w_qkv, L0_conv_b_qkv, L0_conv_temperature, L0_conv_w_proj, L0_conv_b_proj, L1_attn_Wq,
           L1_attn_Wk, L1_attn_Wv, L1_ffn_W1, L1_ffn_b1, L1_ffn_W2, L1_ffn_b2):
    import concourse.bacc as bacc
    from concourse.bass_utils import run_bass_kernel_spmd as run

    (x, wqkv, bqkv, temp, wp, bp, wq, wk, wv, w1, b1, w2, b2) = [np.asarray(a) for a in (
        x, L0_conv_w_qkv, L0_conv_b_qkv, L0_conv_temperature, L0_conv_w_proj, L0_conv_b_proj, L1_attn_Wq,
        L1_attn_Wk, L1_attn_Wv, L1_ffn_W1, L1_ffn_b1, L1_ffn_W2, L1_ffn_b2)]
    B = x.shape[0]
    wt = wqkv.T
    stack = lambda a: np.concatenate([a, a], 0).reshape(3, P, -1).transpose(1, 0, 2)
    v_rows, v_bias = wqkv[2 * C:3 * C], bqkv[2 * C:3 * C][:, None]
    arrays = {
        "x": x.reshape(B, C, NTOK),
        "wa": np.concatenate([wt[0:CH, 0:2 * C], bqkv[None, 0:2 * C]], 0),
        "wb": wt[CH:C, 0:2 * C],
        "wv": np.concatenate([v_rows[:, 0:CH], v_bias, v_rows[:, CH:C]], 1).reshape(2, CH, C + 1).transpose(1, 0, 2),
        "wpt": wp.T.reshape(2, CH, C).transpose(1, 0, 2),
        "bp": bp[None, :],
        "temp": np.repeat(temp.reshape(XH), XD).reshape(2, CH).T,
        "w3": stack(np.concatenate([w[:, D * h:D * h + D] for m in range(3) for w in (wq, wk) for h in (m, 3 + m)]
                                   + [wv], 1)),
        "w1": stack(w1.T),
        "b1": b1.reshape(MH, P).T,
        "w2": w2.T.reshape(MH, P, C).transpose(1, 0, 2),
        "b2": np.broadcast_to(b2, (P, C)),
    }
    arrays = {f"in_{k}": np.ascontiguousarray(a) for k, a in arrays.items()}
    nc = bacc.Bacc("TRN2", target_bir_lowering=False, num_devices=1)
    args = [nc.dram_tensor(k, a.shape, F32, kind="ExternalInput").ap() for k, a in arrays.items()]
    out = nc.dram_tensor("out_y", (B, C, NTOK), F32, kind="ExternalOutput").ap()
    hybrid_kernel(nc, *args, out)
    r = run(nc, [arrays], core_ids=[0])
    return r.results[0]["out_y"].reshape(x.shape)
```

```python
from contextlib import ExitStack

import numpy as np

import concourse.bass as bass
from concourse import mybir

F32 = mybir.dt.float32
F16 = mybir.dt.float16
BF16 = mybir.dt.bfloat16
ALU = mybir.AluOpType
ACT = mybir.ActivationFunctionType
AX = mybir.AxisListType
RMAX = bass.bass_isa.ReduceOp.max
RADD = bass.bass_isa.ReduceOp.add

P = 128
C = 192
CH = C // 2
NTOK = 1024
TT = NTOK // P
XH = 8
XD = C // XH
NH = 6
D = C // NH
HID = 4 * C
MH = HID // P
NGROUPS = 5
LN_EPS = 1e-5
Q_EPS = 1e-5
QB = 128.0
NORM_EPS2 = 1e-24
MASKED = -1e30
WTOP = 16.0

UNITS = NH * TT
U2 = 2 * UNITS
K2 = U2 // 3
TILES = [(0, 7), (1, 6), (2, 5), (3, 4)]
AHEAD = 3
PV_AT, OT_AT, BACK_AT = (8, 11), (9, 12), (11, 13)
LAST_SLOT = 6 * (K2 // 2 - 1) + BACK_AT[1]
RING = 4
STACKS = 8 * 16


def qtile(n):
    return TILES[n // 6 % 4][n % 2]


def triple_of(n):
    return 2 * (n // 6) + n % 2


def unit_of(k, hh):
    return 6 * (k // 2) + k % 2 + 2 * hh


def triples_at(slot, at):
    return [k for k in range(K2) if 6 * (k // 2) + at[k % 2] == slot]


def transposed():
    out = []
    for slot in range(LAST_SLOT + 1):
        m = slot - AHEAD
        if 0 <= m < U2:
            out += [(slot, "p", m, c0, min(4, qtile(m) + 1 - c0)) for c0 in range(0, qtile(m) + 1, 4)]
        out += [(slot, "o", k, 0, 0) for k in triples_at(slot, BACK_AT)]
    return out


CHUNKS = transposed()
PT_PER = len(CHUNKS) // 2
assert len(CHUNKS) % 2 == 0
STEPS = ["xt0", "xt1", "xt2", "xt3", "g0", "g1", "wg0", "wg1", "na", "rb", "u", "mt", "t0", "t1", "t2", "t3",
         "z0", "z1", "z2", "z3", "qk0", "qk1", "qk2", "qk3", "qk4", "qk5", "v0", "v1", "v2", "v3"]
FREES = {"wg0": 2, "wg1": 2, "mt": 2}
LN_PER = 26
JR = 8
XSOFT = 9
FRONT_STEPS = len(STEPS)
NEEDS = {"g0": "xt3", "wg0": "g1", "na": "wg1", "mt": "u", "t0": "mt", "qk0": "z3"}


def bank_of(step):
    return STEPS.index(step) % 2


def freed(step):
    i = STEPS.index(step)
    return sum(FREES.get(s, 1) for s in STEPS[i % 2:i + 1:2])


FRONT_FREES = [freed(STEPS[-2]), freed(STEPS[-1])]
assert FRONT_STEPS % 2 == 0


SLOTS = {"xt0": 0, "xt1": 1, "xt2": 2, "xt3": 4, "g0a": 5, "g0": 6, "g1a": 7, "g1": 8, "wg0": 9, "wg1": 10,
         "na": 11, "rb": 15, "u": 18, "mt": 19, "t0": 20, "t1": 21, "t2": 22, "t3": 23, "z0": 31, "z1": 32,
         "z2": 33, "z3": 34, "qk0": 35, "qk1": 36, "qk2": 37, "qk3": 38, "qk4": 39, "qk5": 40, "v0": 41, "v1": 42,
         "v2": 43, "v3": 44}
SMALL_SLOTS = {"norms": 12, "rdiag": 13, "logits": 16, "xexp": 17, "attn": 17.5, "ln_stats0": 22, "ln_stats1": 25,
               "ln_norm0": 27, "ln_norm1": 28, "ln_round0": 28.5, "ln_round1": 29}


def hybrid_kernel(nc, x, wa, wb, wv, wpt, bp, temp, w3, w1, b1, w2, b2, out):
    B = x.shape[0]
    GS = B // NGROUPS
    assert GS % 2 == 0 and B - NGROUPS * GS == 2

    ctx = ExitStack()
    with ctx:
        def sb(name, shape, dt=F32):
            return ctx.enter_context(nc.sbuf_tensor(name, shape, dt))

        def sem(name):
            return ctx.enter_context(nc.semaphore(name))

        ident = sb("ident", [P, P])
        ident16 = sb("ident16", [P, P], F16)
        identb = sb("identb", [P, P], BF16)
        causal = sb("causal", [P, P], BF16)
        ones = sb("ones", [CH + 1, CH])
        epst = sb("epst", [P, TT])
        halfneg = sb("halfneg", [P, TT])
        WT = sb("WT", [CH + 1, 2, 2 * C])
        WV = sb("WV", [CH, 2, C + 1])
        WPT = sb("WPT", [CH, 2, C])
        IADD = sb("IADD", [CH + 1, 2, C])
        blockmask = sb("blockmask", [CH, 2, CH])
        tempc = sb("tempc", [CH, 2])
        W3h = sb("W3h", [P, 3, 3 * C], F16)
        W3l = sb("W3l", [P, 3, 3 * C], F16)
        W1b = sb("W1b", [P, 3, HID], F16)
        W2b = sb("W2b", [P, MH, C], F16)
        B1 = sb("B1", [P, MH])
        B2 = sb("B2", [P, C])
        sc = sb("sc", [P, 64])
        X = sb("X", [CH + 1, 2, NTOK])
        XT = sb("XT", [P, TT, C + 1])
        Z = XT[:, :, 0:C]
        zt = sb("zt", [P, 3, NTOK], F16)
        small = zt[:, :, :].rearrange("p a b -> p (a b)").bitcast(F32)
        G = small[0:CH + 1, 0:2 * (C + 1)].rearrange("p (a b) -> p a b", a=2)
        TK = small[0:CH + 1, 386:386 + 2 * C].rearrange("p (a b) -> p a b", a=2)
        U = small[0:CH, 770:770 + 2 * C].rearrange("p (a b) -> p a b", a=2)
        LOG = small[0:CH, 1154:1154 + 2 * CH].rearrange("p (a b) -> p a b", a=2)
        NK = sb("NK", [CH, 4])
        RD = sb("RD", [CH, 2, CH])
        ATT = RD
        MT = sb("MT", [CH + 1, 2, C])
        hi_z = sb("hi_z", [P, 3 * NTOK], F16)
        QKH = hi_z[:, :].rearrange("p (a b) -> p a b", a=3)
        zcat = hi_z[:, :].rearrange("p (a b) -> p a b", a=TT)
        PROD = hi_z[0:CH + 1, :].bitcast(F32)[:, 0:4 * C].rearrange("p (a b) -> p a b", a=2)
        T0 = sb("T0", [P, 2, TT, C])
        QS0 = sb("QS0", [P, NH, NTOK], F16)
        KS0 = sb("KS0", [P, NH, NTOK], F16)
        V0 = sb("V0", [P, TT, C])
        odd = sb("odd", [P, GS * 3 * NTOK if GS * 3 * NTOK > 18432 else 18432], F16)
        QS1 = odd[:, 0:6144].rearrange("p (a b) -> p a b", a=NH)
        KS1 = odd[:, 6144:12288].rearrange("p (a b) -> p a b", a=NH)
        QKL = odd[:, 12288:15360].rearrange("p (a b) -> p a b", a=3)
        V1 = odd[:, 15360:18432].bitcast(F32).rearrange("p (a b) -> p a b", a=TT)
        QS, KS, V = [QS0, QS1], [KS0, KS1], [V0, V1]
        Z2 = odd[:, 0:GS * 3 * NTOK].rearrange("p (b h j n) -> p b h j n", b=GS, h=2, j=3)
        Y2 = odd[:, 0:GS * 3 * NTOK].bitcast(F32).rearrange("p (b h n) -> p b h n", b=GS, h=2)
        T1 = sb("T1", [P, GS, TT, C])
        T1H = T1[:, :, :, :].rearrange("p b (h t) c -> p b h (t c)", h=2)
        work = sb("work", [P, 9216])
        PS = [work[:, 0:1024].rearrange("p (a b) -> p a b", a=2), work[:, 1024:3072].rearrange("p (a b) -> p a b", a=2)]
        PTS = [work[:, 3072:5120].rearrange("p (a b) -> p a b", a=RING),
               work[:, 5120:9216].rearrange("p (a b) -> p a b", a=RING)]
        H = work[:, 0:512 * MH].rearrange("p (m n) -> p m n", m=MH)
        HS = work[:, 512 * MH:512 * 3 * MH].bitcast(F16).rearrange("p (h s m n) -> p h s m n", h=2, s=2, m=MH)
        JUNK = work[:, 0:512 * JR].rearrange("p (a b) -> p a b", a=JR)
        OS = work[0:CH, 0:2048].rearrange("p (h c n) -> p h c n", h=2, c=2)
        OT = work[:, 2048:2048 + 2 * 4 * C].rearrange("p (h n) -> p h n", h=2)
        oT = sb("oT", [CH, 2, P])
        rowsum = sb("rowsum", [P, U2])
        nmax = sb("nmax", [P, U2])
        stats = sb("stats", [P, TT, 6])
        mv = sb("mv", [P, TT, 2])
        rstd = sb("rstd", [P, TT])
        fin = sb("fin", [P, CH])
        gm = sb("gm", [P, 16])
        scratch = odd[:, :].bitcast(F32)
        W3f = scratch[:, 0:1728].rearrange("p (a b) -> p a b", a=3)
        W1f = scratch[:, 1728:4032].rearrange("p (a b) -> p a b", a=3)
        W1c = scratch[:, 4032:6336].rearrange("p (a b) -> p a b", a=3)
        W2f = scratch[:, 6336:7488].rearrange("p (a b) -> p a b", a=MH)
        W2c = scratch[:, 7488:8640].rearrange("p (a b) -> p a b", a=MH)

        amax, wscale, vback = sc[:, 0:3], sc[:, 3:6], sc[:, 6:7]
        qkback, qkprod = sc[:, 7:8], sc[:, 8:9]
        sum1, sum2 = sc[:, 10:15], sc[:, 15:20]
        run1, run2, gam1, gam2 = sc[:, 20:21], sc[:, 21:22], sc[:, 22:23], sc[:, 23:24]
        ge, gr, r1, c1 = sc[:, 24:25], sc[:, 25:26], sc[:, 26:27], sc[:, 27:28]
        ge2, gr2, r2, c2, c2n = sc[:, 28:29], sc[:, 29:30], sc[:, 30:31], sc[:, 31:32], sc[:, 32:33]
        clip_hi, clip_lo, rb1 = sc[:, 33:39], sc[:, 39:45], sc[:, 45:51]
        rqt = sc[0:CH, 51:53]
        xmax, xsum = sc[0:CH, 53:55], sc[0:CH, 55:57]
        rsum3 = sc[:, 57:60]
        xrec = sc[0:CH, 60:62]
        half = sc[:, 62:63]

        S = ctx.enter_context(nc.psum_tensor("S", [P, 2, 1024], F32))
        PT = [ctx.enter_context(nc.psum_tensor(f"PT{i}", [P, 512], F32)) for i in range(2)]
        OUT = ctx.enter_context(nc.psum_tensor("OUT", [P, 512], F32))
        FR = ctx.enter_context(nc.psum_tensor("FR", [P, 512], F32))
        FB = [FR[:, :], S[:, 0, 512:1024]]
        Y = [S[:, i // 2, 512 * (i % 2):512 * (i % 2) + 512] for i in range(4)]
        ZP = [FR[:, :], OUT[:, :]]

        w_in = sem("w_in")
        bias_in = sem("bias_in")
        cst_made = sem("cst_made")
        prep = sem("prep")
        prep_all = sem("prep_all")
        w_ready = sem("w_ready")
        x_in = sem("x_in")
        front_full = sem("front_full")
        front_free = [sem(f"front_free{i}") for i in range(2)]
        norm2_made = sem("norm2_made")
        rnorm_made = sem("rnorm_made")
        xsoft = sem("xsoft")
        xexp_made = sem("xexp_made")
        ln_step = sem("ln_step")
        rstd_made = sem("rstd_made")
        zlo_made = sem("zlo_made")
        qkhi_made = sem("qkhi_made")
        qklo_made = sem("qklo_made")
        stacked = [sem(f"stacked{i}") for i in range(2)]
        scores_full = sem("scores_full")
        max_made = sem("max_made")
        exp_made = sem("exp_made")
        pt_full = [sem(f"pt_full{i}") for i in range(2)]
        pt_free = [sem(f"pt_free{i}") for i in range(2)]
        pv_made = sem("pv_made")
        oT_made = sem("oT_made")
        t1_step = sem("t1_step")
        ln2_step = sem("ln2_step")
        rstd2_made = sem("rstd2_made")
        z2lo_made = sem("z2lo_made")
        z2t_full = sem("z2t_full")
        z2t_made = sem("z2t_made")
        y1_full = sem("y1_full")
        abs_made = sem("abs_made")
        max1_step = sem("max1_step")
        gam1_made = sem("gam1_made")
        quant1_step = sem("quant1_step")
        y_full = sem("y_full")
        clip_made = sem("clip_made")
        gelu_made = sem("gelu_made")
        hhi_made = sem("hhi_made")
        hlo_made = sem("hlo_made")
        y2_full = sem("y2_full")
        y2_made = sem("y2_made")
        max2_step = sem("max2_step")
        gam2_made = sem("gam2_made")
        quant2_step = sem("quant2_step")
        o_step = sem("o_step")
        ot_full = sem("ot_full")
        os_made = sem("os_made")
        stored = [sem(f"stored{i}") for i in range(2)]
        passed = sem("passed")

        def groups(e, body, tail):
            with e.Fori(0, NGROUPS) as g:
                with e.Fori(0, GS // 2) as p:
                    body(e.snap(g * (GS // 2) + p), p)
                tail(g)

        LAST = NGROUPS * GS // 2

        def after(pair, u, per, n):
            return pair * (2 * per) + (u * per + n)

        def wait_freed(e, pair, u, step, less=0):
            b = bank_of(step)
            e.wait_ge(front_free[b], after(pair, u, FRONT_FREES[b], freed(step) - less))

        def of_pair(pair, per, n):
            return pair * per + n

        def fronts_at(slot, run, parts, fronts):
            for u in range(fronts):
                for name, at in parts:
                    if UNITS * u + int(at) == slot:
                        run(name, u)

        def by_act(i, chunk):
            return chunk[1] == "p" and chunk[3] > 0

        def pt_copy(eng, copy, pair, i):
            _, _, m, c0, k = CHUNKS[i]
            eng.wait_ge(pt_full[i % 2], of_pair(pair, PT_PER, i // 2 + 1))
            if m >= 2 * RING:
                eng.wait_ge(pv_made, of_pair(pair, K2, triple_of(m - 2 * RING) + 1))
            copy(PTS[m % 2][:, m // 2 % RING, P * c0:P * (c0 + k)], PT[i % 2][:, 0:P * k]).then_inc(pt_free[i % 2], 1)

        def chunks_at(slot):
            return [(i, c) for i, c in enumerate(CHUNKS) if c[0] == slot]

        def alone(e):
            e.sem_inc(passed, 1)

        block = ctx.enter_context(nc.Block())

        @block.sync
        def _(sp):
            for dst, src in ((WT[0:CH + 1, 0, :], wa), (WT[0:CH, 1, :], wb), (WV[:, :, :], wv), (WPT[:, :, :], wpt),
                             (tempc[:, :], temp), (W3f[:, :, :], w3), (W1f[:, :, :], w1), (B1[:, :], b1),
                             (W2f[:, :, :], w2), (B2[:, :], b2)):
                sp.dma_start(dst, src).then_inc(w_in, 16)
            sp.wait_ge(cst_made, 11)
            sp.dma_start(IADD[CH:CH + 1, 0, :], bp).then_inc(bias_in, 16)

            def load_x(b):
                sp.dma_start(X[0:CH, :, :], x[b].rearrange("(c p) n -> p c n", p=CH)).then_inc(x_in, 16)

            def front(pair, u, more):
                if more:
                    sp.wait_ge(front_full, after(pair, u, FRONT_STEPS, STEPS.index("t3") + 1))
                    load_x(pair * 2 + (u + 1))
                sp.wait_ge(qklo_made, after(pair, u, 6, 6))
                for grp in range(2):
                    for r, stack, srcs in ((grp, QS, (QKH, QKL, QKH, QKL)), (2 + grp, KS, (QKH, QKH, QKL, QKL))):
                        for part in range(4):
                            sp.dma_start(stack[u % 2][32 * part:32 * part + 32, 3 * grp:3 * grp + 3, :],
                                         srcs[part][32 * r:32 * r + 32, :, :]).then_inc(stacked[grp], 16)

            def store(b, hf, n):
                sp.wait_ge(os_made, n)
                sp.dma_start(out[b].rearrange("(c p) n -> p c n", p=CH)[:, :, 512 * hf:512 * hf + 512],
                             OS[:, hf, :, :]).then_inc(stored[hf], 16)

            for hf in range(2):
                sp.sem_inc(stored[hf], 16)
            load_x(0)
            front(0, 0, True)

            def pair_body(pair, p):
                for u in range(2):
                    front(pair, u + 1, True)

            def group_tail(g):
                with sp.Fori(0, GS) as b:
                    for hf in range(2):
                        store(g * GS + b, hf, g * (2 * GS) + b * 2 + (hf + 3))

            groups(sp, pair_body, group_tail)
            front(LAST, 1, False)
            for u in range(2):
                for hf in range(2):
                    store(2 * LAST + u, hf, 4 * LAST + 2 * u + hf + 3)
            for hf in range(2):
                sp.wait_ge(stored[hf], 16 * (B + 1))

        @block.gpsimd
        def _(pool):
            pool.memset(ident[:, :], 0.0).then_inc(cst_made, 1)
            pool.memset(causal[:, :], 0.0).then_inc(cst_made, 1)
            pool.memset(IADD[:, :, :], 0.0).then_inc(cst_made, 1)
            pool.memset(blockmask[:, :, :], 0.0).then_inc(cst_made, 1)
            pool.memset(ones[:, :], 1.0).then_inc(cst_made, 1)
            pool.memset(halfneg[:, :], -0.5).then_inc(cst_made, 1)
            pool.memset(epst[:, :], LN_EPS).then_inc(cst_made, 1)
            pool.wait_ge(cst_made, 7)
            pool.affine_select(out=ident[:, :], in_=ident[:, :], compare_op=ALU.not_equal, fill=1.0, base=0,
                               pattern=[[-1, P]], channel_multiplier=1).then_inc(cst_made, 1)
            pool.affine_select(out=causal[:, :], in_=causal[:, :], compare_op=ALU.is_ge, fill=MASKED, base=0,
                               pattern=[[-1, P]], channel_multiplier=1).then_inc(cst_made, 1)
            pool.affine_select(out=IADD[0:CH, :, :], in_=IADD[0:CH, :, :], compare_op=ALU.not_equal, fill=1.0,
                               base=0, pattern=[[CH, 2], [-1, C]], channel_multiplier=1).then_inc(cst_made, 1)
            bm = blockmask[:, :, :].rearrange("p m (h d) -> p m h d", d=XD)
            pool.affine_select(out=bm, in_=bm, compare_op=ALU.is_ge, fill=MASKED, base=0,
                               pattern=[[0, 2], [-XD, CH // XD], [0, XD]], channel_multiplier=1).then_inc(cst_made, 1)
            pool.wait_ge(cst_made, 11)
            pool.affine_select(out=bm, in_=bm, compare_op=ALU.is_ge, fill=MASKED, base=XD - 1,
                               pattern=[[0, 2], [XD, CH // XD], [0, XD]], channel_multiplier=-1).then_inc(cst_made, 1)
            pool.tensor_copy(ident16[:, :], ident[:, :]).then_inc(cst_made, 1)
            pool.tensor_copy(identb[:, :], ident[:, :]).then_inc(cst_made, 1)
            pool.wait_ge(prep, 3)
            pool.partition_all_reduce(amax, sc[:, 33:36], P, RMAX).then_inc(prep_all, 1)
            pool.wait_ge(prep, 3 + 2 * NGROUPS)
            pool.partition_all_reduce(sc[:, 10:20], sc[:, 36:46], P, RADD).then_inc(prep_all, 1)
            pool.wait_ge(prep, 3 + 2 * NGROUPS + 3)
            pool.tensor_tensor(qkback, qkprod, half, ALU.pow).then_inc(prep_all, 1)

            def front(pair, u):
                pool.wait_ge(norm2_made, after(pair, u, 1, 1))
                pool.tensor_tensor(NK[:, :], NK[:, :], halfneg[0:CH, 0:4], ALU.pow).then_inc(rnorm_made, 1)
                pool.wait_ge(ln_step, after(pair, u, LN_PER, 16))
                pool.tensor_tensor(rstd[:, :], mv[:, :, 1], epst[:, :], ALU.add).then_inc(rstd_made, 1)
                pool.wait_ge(rstd_made, after(pair, u, 2, 1))
                pool.tensor_tensor(rstd[:, :], rstd[:, :], halfneg[:, 0:TT], ALU.pow).then_inc(rstd_made, 1)
                for hf in range(2):
                    pool.wait_ge(ln_step, after(pair, u, LN_PER, 25 + hf))
                    ts = slice(4 * hf, 4 * hf + 4)
                    pool.tensor_tensor(zcat[:, ts, C:2 * C], Z[:, ts, :], zcat[:, ts, 0:C],
                                       ALU.subtract).then_inc(zlo_made, 1)

            front(0, 0)

            def pair_body(pair, p):
                for u in range(2):
                    front(pair, u + 1)

            def group_tail(g):
                with pool.Fori(0, GS) as b:
                    ab = pool.snap(g * GS + b)
                    pool.wait_ge(ln2_step, ab * LN_PER + 16)
                    pool.tensor_tensor(rstd[:, :], mv[:, :, 1], epst[:, :], ALU.add).then_inc(rstd2_made, 1)
                    pool.wait_ge(rstd2_made, ab * 2 + 1)
                    pool.tensor_tensor(rstd[:, :], rstd[:, :], halfneg[:, 0:TT], ALU.pow).then_inc(rstd2_made, 1)
                    for hf in range(2):
                        pool.wait_ge(ln2_step, ab * LN_PER + (25 + hf))
                        ts = slice(4 * hf, 4 * hf + 4)
                        pool.tensor_tensor(zcat[:, ts, C:2 * C], Z[:, ts, :], zcat[:, ts, 0:C],
                                           ALU.subtract).then_inc(z2lo_made, 1)
                pool.wait_ge(max1_step, (g + 1) * (GS * 14 + 1))
                alone(pool)
                pool.partition_all_reduce(gam1, run1, P, RMAX).then_inc(gam1_made, 1)
                with pool.Fori(0, GS) as b:
                    ab = pool.snap(g * GS + b)
                    for i in range(2 * MH):
                        pool.wait_ge(hhi_made, ab * 12 + (i + 1))
                        hs = HS[:, i // MH, :, i % MH, :]
                        pool.tensor_tensor(hs[:, 1, :], H[:, i % MH, :], hs[:, 0, :], ALU.subtract).then_inc(hlo_made, 1)
                pool.wait_ge(max2_step, (g + 1) * (GS * 4 + 1))
                alone(pool)
                pool.partition_all_reduce(gam2, run2, P, RMAX).then_inc(gam2_made, 1)

            groups(pool, pair_body, group_tail)
            front(LAST, 1)

        @block.tensor
        def _(pe):
            mm = nc.tensor.matmul
            tr = nc.tensor.transpose
            pe.wait_ge(cst_made, 14)
            pe.wait_ge(w_in, 16 * 10)
            pe.wait_ge(w_ready, 1)

            def front_part(name, pair, u):
                FR = FB[bank_of({"g0a": "g0", "g1a": "g1"}.get(name, name))]
                if name not in ("g0", "g1"):
                    step = {"g0a": "g0", "g1a": "g1"}.get(name, name)
                    i = STEPS.index(step)
                    if i >= 2:
                        wait_freed(pe, pair, u, STEPS[i - 2])
                    elif u or not isinstance(pair, int):
                        wait_freed(pe, pair, u - 1, STEPS[i - 2])
                    if step in NEEDS:
                        wait_freed(pe, pair, u, NEEDS[step])
                if name.startswith("xt"):
                    k = int(name[2:])
                    if k == 0:
                        pe.wait_ge(x_in, after(pair, u, 16, 16))
                    for t in range(2):
                        cols = slice((2 * k + t) * P, (2 * k + t + 1) * P)
                        o = t * (C + 1)
                        tr(FR[:, o:o + CH + 1], X[0:CH + 1, 0, cols], ident[0:CH + 1, 0:CH + 1])
                        last = tr(FR[:, o + CH + 1:o + C + 1], X[0:CH, 1, cols], ident[0:CH, 0:CH])
                elif name in ("g0a", "g0", "g1a", "g1"):
                    c0, m = (0, CH + 1) if name[1] == "0" else (CH + 1, CH)
                    o = 0
                    for t in (range(0, 4) if name.endswith("a") else range(4, 8)):
                        last = mm(FR[0:m, o:o + C + 1], XT[:, t, c0:c0 + m], XT[:, t, :],
                                  start=(t == 0), stop=(t == TT - 1))
                    if name.endswith("a"):
                        return
                elif name in ("wg0", "wg1"):
                    c0, m = (0, CH + 1) if name == "wg0" else (CH + 1, CH)
                    mm(FR[0:m, 0:2 * C], G[0:CH + 1, 0, c0:c0 + m], WT[0:CH + 1, 0, :], start=True, stop=False)
                    last = mm(FR[0:m, 0:2 * C], G[0:CH, 1, c0:c0 + m], WT[0:CH, 1, :], start=False, stop=True)
                elif name == "na":
                    for j in range(4):
                        for c, m in ((0, CH + 1), (1, CH)):
                            mm(FR[0:CH, C + j:C + j + 1], PROD[0:m, c, CH * j:CH * j + CH], ones[0:m, 0:1],
                               start=(c == 0), stop=(c == 1))
                    for j in range(2):
                        for c, m in ((0, CH + 1), (1, CH)):
                            last = mm(FR[0:CH, 256 + CH * j:256 + CH * j + CH], WT[0:m, c, CH * j:CH * j + CH],
                                      TK[0:m, c, CH * j:CH * j + CH], start=(c == 0), stop=(c == 1))
                elif name == "rb":
                    pe.wait_ge(xsoft, after(pair, u, XSOFT, 2))
                    last = mm(FR[0:CH, 0:C], ones[0:CH, :], RD[:, :, :].rearrange("p a b -> p (a b)"),
                              start=True, stop=True)
                elif name == "u":
                    pe.wait_ge(xsoft, after(pair, u, XSOFT, XSOFT))
                    for j in range(2):
                        last = mm(FR[0:CH, C * j:C * j + C], ATT[:, j, :], WPT[:, j, :], start=True, stop=True)
                elif name == "mt":
                    for c, c0, m in ((0, 0, CH + 1), (1, CH + 1, CH)):
                        for j in range(2):
                            last = mm(FR[0:m, C * c:C * c + C], WV[:, j, c0:c0 + m], U[:, j, :],
                                      start=(j == 0), stop=(j == 1))
                elif name[0] == "t":
                    k = int(name[1:])
                    for t in range(2):
                        cols = slice((2 * k + t) * P, (2 * k + t + 1) * P)
                        mm(FR[:, C * t:C * t + C], X[0:CH + 1, 0, cols], MT[0:CH + 1, 0, :], start=True, stop=False)
                        last = mm(FR[:, C * t:C * t + C], X[0:CH, 1, cols], MT[0:CH, 1, :], start=False, stop=True)
                elif name[0] == "z":
                    k = int(name[1:])
                    if k % 2 == 0:
                        pe.wait_ge(zlo_made, after(pair, u, 2, k // 2 + 1))
                    last = turn_z(FR, k)
                elif name.startswith("qk"):
                    i = int(name[2:])
                    m, hf = i // 2, i % 2
                    for j in range(3):
                        for w in (W3h, W3l):
                            last = mm(FR, w[:, j, P * m:P * m + P], zt[:, j, 512 * hf:512 * hf + 512],
                                      start=(j == 0 and w is W3h), stop=(j == 2 and w is W3l))
                else:
                    k = int(name[1:])
                    for t in range(2):
                        for j in range(3):
                            for w in (W3h, W3l):
                                last = mm(FR[:, C * t:C * t + C], zt[:, j, (2 * k + t) * P:(2 * k + t + 1) * P],
                                          w[:, j, 2 * C:3 * C], start=(j == 0 and w is W3h),
                                          stop=(j == 2 and w is W3l))
                last.then_inc(front_full, 1)

            def turn_z(bank, k):
                v = bank.bitcast(F16).rearrange("p (j n) -> p j n", j=4)
                for t in range(2):
                    for j in range(3):
                        last = tr(v[:, j, P * t:P * t + P], zcat[:, 2 * k + t, P * j:P * j + P], ident16[:, :])
                return last

            pe.sem_inc(ot_full, 2)
            pe.sem_inc(y2_full, 4)
            for name in SLOTS:
                front_part(name, 0, 0)

            def attention(pair, fronts):
                for n in range(LAST_SLOT + 1):
                    if n < U2:
                        u, h, qt = n // UNITS, 3 * (n % UNITS // 24) + n % 6 // 2, qtile(n)
                        if n % 24 == 0:
                            pe.wait_ge(stacked[n % UNITS // 24], after(pair, u, STACKS, STACKS))
                        if n >= 2:
                            pe.wait_ge(exp_made, of_pair(pair, U2, n - 1))
                        q = QS[u][:, h, P * qt:P * qt + P]
                        w = P * (qt + 1)
                        for c0 in range(0, w, 512):
                            mm(S[:, n % 2, c0:min(w, c0 + 512)], q, KS[u][:, h, c0:min(w, c0 + 512)],
                               start=True, stop=c0 + 512 < w)
                        mm(S[:, n % 2, w - P:w], identb[:, :], causal[:, :], start=False,
                           stop=True).then_inc(scores_full, 1)
                    for i, (_, kind, m, c0, k) in chunks_at(n):
                        bank = PT[i % 2]
                        if kind == "p" and c0 == 0:
                            pe.wait_ge(exp_made, of_pair(pair, U2, m + 1))
                        if kind == "p":
                            if i >= 2:
                                pe.wait_ge(pt_free[i % 2], of_pair(pair, PT_PER, i // 2))
                            for j in range(c0, c0 + k):
                                last = tr(bank[:, P * (j - c0):P * (j - c0) + P], PS[m % 2][:, m // 2 % 2, P * j:P * j + P],
                                          ident[:, :])
                            last.then_inc(pt_full[i % 2], 1)
                    for k in triples_at(n, PV_AT):
                        u, grp, qt = k // (K2 // 2), k % (K2 // 2) // 8, qtile(unit_of(k, 0))
                        done = [i for i, c in enumerate(CHUNKS) if c[1] == "p" and c[2] <= unit_of(k, 2)]
                        for b in range(2):
                            pe.wait_ge(pt_free[b], of_pair(pair, PT_PER, max(i for i in done if i % 2 == b) // 2 + 1))
                        if k % (K2 // 2) == 0:
                            for step in STEPS[-2:]:
                                wait_freed(pe, pair, u, step)
                        if k:
                            pe.wait_ge(oT_made, of_pair(pair, K2, k))
                        for j in range(qt + 1):
                            for hh in range(3):
                                h = 3 * grp + hh
                                last = mm(OUT[32 * hh:32 * hh + 32, 0:P],
                                          V[u][:, j, D * h:D * h + D], PTS[k % 2][:, unit_of(k, hh) // 2 % RING, P * j:P * j + P],
                                          start=(j == 0), stop=(j == qt), tile_position=(0, 32 * hh))
                        last.then_inc(pv_made, 1)
                    for i, (_, kind, k, _, _) in chunks_at(n):
                        if kind == "o":
                            pe.wait_ge(pt_free[i % 2], of_pair(pair, PT_PER, i // 2))
                            pe.wait_ge(oT_made, of_pair(pair, K2, k + 1))
                            tr(PT[i % 2][:, 0:CH], oT[:, k % 2, :], ident[0:CH, 0:CH]).then_inc(pt_full[i % 2], 1)
                    fronts_at(n, lambda name, u: front_part(name, pair, u + 1), SLOTS.items(), fronts)

            def ffn1(rhs, bank, i):
                for j in range(3):
                    last = mm(bank, W1b[:, j, P * (i % 6):P * (i % 6) + P], rhs[:, j, :],
                              start=(j == 0), stop=(j == 2))
                return last

            def turn_out(src, hf):
                for c in range(2):
                    for t in range(4):
                        o = 512 * c + P * t
                        last = tr(S[0:CH, hf, o:o + P], src(t, c), ident[:, :])
                return last

            def pair_body(pair, p):
                attention(pair, 2)

            def group_tail(g):
                nb = g + 1
                pe.wait_ge(t1_step, nb * (GS * UNITS))
                for i in range(2):
                    pe.wait_ge(front_free[i], nb * (GS * FRONT_FREES[i]) + FRONT_FREES[i])
                for st in stacked:
                    pe.wait_ge(st, nb * (GS * STACKS) + STACKS)
                alone(pe)

                def turn_z2(ab, abs_before):
                    for k in range(4):
                        if k % 2 == 0:
                            pe.wait_ge(z2lo_made, ab * 2 + (k // 2 + 1))
                        if k >= 2:
                            pe.wait_ge(z2t_made, ab * 4 + (k - 1))
                        turn_z(ZP[k % 2], k).then_inc(z2t_full, 1)
                    if abs_before is not None:
                        pe.wait_ge(abs_made, abs_before)
                        alone(pe)

                def y1(b, ab):
                    for i in range(12):
                        if i % 6 == 0:
                            pe.wait_ge(z2t_made, ab * 4 + (2 + 2 * (i // 6)))
                        if i >= 4:
                            pe.wait_ge(abs_made, ab * 12 + (i - 3))
                        ffn1(Z2[:, b, i // 6], Y[i % 4], i).then_inc(y1_full, 1)

                turn_z2(g * GS, None)
                with pe.Fori(0, GS - 1) as b:
                    ab = pe.snap(g * GS + b)
                    y1(b, ab)
                    turn_z2(pe.snap(ab + 1), ab * 12 + 12)
                y1(GS - 1, g * GS + (GS - 1))
                pe.wait_ge(abs_made, nb * (GS * 12))
                alone(pe)

                def y(b, ab, hf, clips):
                    for m in range(MH):
                        if clips is not None or m >= 4:
                            pe.wait_ge(clip_made, (ab * 12 if clips is None else clips) + (m - 3))
                        ffn1(Z2[:, b, hf], Y[(MH * hf + m) % 4], m).then_inc(y_full, 1)

                def y2(ab, hf):
                    pe.wait_ge(hlo_made, ab * 12 + MH * (hf + 2))
                    for tp in range(2 * hf, 2 * hf + 2):
                        if hf:
                            pe.wait_ge(y2_made, ab * 4 + (tp - 1))
                        for t in range(2):
                            o = P * (2 * (tp % 2) + t)
                            for m in range(MH):
                                for part in range(2):
                                    last = mm(PT[tp % 2][:, C * t:C * t + C], HS[:, hf, part, m, o:o + P], W2b[:, m, :],
                                              start=(m == 0 and part == 0), stop=(m == MH - 1 and part == 1))
                        last.then_inc(y2_full, 1)

                y(0, g * GS, 0, None)
                with pe.Fori(0, GS - 1) as b:
                    ab = pe.snap(g * GS + b)
                    y(b, ab, 1, ab * 12 + MH)
                    y2(ab, 0)
                    y(pe.snap(b + 1), None, 0, ab * 12 + 2 * MH)
                    y2(ab, 1)
                ab = g * GS + (GS - 1)
                y(GS - 1, ab, 1, ab * 12 + MH)
                y2(ab, 0)
                y2(ab, 1)
                with pe.Fori(0, GS) as b:
                    ab = pe.snap(g * GS + b)
                    for hf in range(2):
                        pe.wait_ge(o_step, ab * 4 + (hf + 3))
                        pe.wait_ge(os_made, ab * 2 + (hf + 1))
                        turn_out(lambda t, c: OT[:, hf, C * t + CH * c:C * t + CH * c + CH], hf).then_inc(ot_full, 1)
                pe.wait_ge(os_made, nb * (2 * GS) + 2)

            groups(pe, pair_body, group_tail)
            attention(LAST, 1)
            pe.wait_ge(t1_step, UNITS * B)
            for u in range(2):
                for hf in range(2):
                    pe.wait_ge(os_made, 4 * LAST + 2 * u + hf + 1)
                    turn_out(lambda t, c: T1[:, u, 4 * hf + t, CH * c:CH * c + CH], hf).then_inc(ot_full, 1)

        @block.scalar
        def _(act):
            A = nc.scalar.activation
            act.wait_ge(w_ready, 1)
            act.sem_inc(os_made, 2)
            act.sem_inc(hlo_made, MH)

            def front_part(name, pair, u):
                f = u % 2
                FR = FB[bank_of(name)] if name in STEPS else None
                if name in ("g0a", "g1a", "na", "rb"):
                    return
                if name == "xexp":
                    act.wait_ge(xsoft, after(pair, u, XSOFT, 6))
                    for j in range(2):
                        A(ATT[:, j, :], LOG[:, j, :], ACT.Exp, bias=xmax[:, j:j + 1],
                          accum_out=xsum[:, j:j + 1]).then_inc(xexp_made, 1)
                    return
                if name not in STEPS or name == "mt":
                    return
                act.wait_ge(front_full, after(pair, u, FRONT_STEPS, STEPS.index(name) + 1))
                if name.startswith("xt"):
                    k = int(name[2:])
                    o = A(XT[:, 2 * k:2 * k + 2, :], FR[:, 0:2 * (C + 1)].rearrange("p (t c) -> p t c", t=2), ACT.Copy)
                elif name in ("g0", "g1"):
                    c, m = int(name[1]), CH + 1 - int(name[1])
                    o = A(G[0:m, c, :], FR[0:m, 0:C + 1], ACT.Copy)
                elif name in ("wg0", "wg1"):
                    c, m = int(name[2]), CH + 1 - int(name[2])
                    wait_freed(act, pair, u, name, 1)
                    o = A(TK[0:m, c, :], FR[0:m, C:2 * C], ACT.Copy)
                elif name == "u":
                    o = A(U[:, :, :], FR[0:CH, 0:2 * C].rearrange("p (a b) -> p a b", a=2), ACT.Copy)
                elif name[0] == "t":
                    k = int(name[1:])
                    o = A(T0[:, f, 2 * k:2 * k + 2, :], FR[:, 0:2 * C].rearrange("p (a b) -> p a b", a=2), ACT.Copy)
                elif name[0] == "z":
                    k = int(name[1:])
                    v = FR.bitcast(F16).rearrange("p (j n) -> p j n", j=4)
                    o = A(zt[:, :, 256 * k:256 * k + 256], v[:, 0:3, :], ACT.Copy)
                elif name.startswith("qk"):
                    i = int(name[2:])
                    A(QKH[:, i // 2, 512 * (i % 2):512 * (i % 2) + 512], FR, ACT.Copy,
                      scale=qkback).then_inc(qkhi_made, 1)
                    return
                else:
                    k = int(name[1:])
                    o = A(V[f][:, 2 * k:2 * k + 2, :], FR[:, 0:2 * C].rearrange("p (a b) -> p a b", a=2), ACT.Copy,
                          scale=vback)
                o.then_inc(front_free[bank_of(name)], 1)

            order = list(SLOTS.items()) + [("xexp", SMALL_SLOTS["xexp"])]
            order.sort(key=lambda a: a[1])
            for name, _ in order:
                front_part(name, 0, 0)

            def attention(pair, fronts):
                for n in range(LAST_SLOT + 1):
                    for k in triples_at(n, OT_AT):
                        act.wait_ge(pv_made, of_pair(pair, K2, k + 1))
                        if k >= 2:
                            act.wait_ge(t1_step, of_pair(pair, 3 * K2, 3 * (k - 2) + 2))
                        A(oT[:, k % 2, :], OUT[0:CH, 0:P], ACT.Copy).then_inc(oT_made, 1)
                    if n < U2:
                        act.wait_ge(max_made, of_pair(pair, U2, n + 1))
                        if n >= 4:
                            i = max(i for i, c in enumerate(CHUNKS) if c[1] == "p" and c[2] == n - 4)
                            act.wait_ge(pt_full[i % 2], of_pair(pair, PT_PER, i // 2 + 1))
                        w = P * (qtile(n) + 1)
                        A(PS[n % 2][:, n // 2 % 2, 0:w], S[:, n % 2, 0:w], ACT.Exp, bias=nmax[:, n:n + 1],
                          accum_out=rowsum[:, n:n + 1]).then_inc(exp_made, 1)
                    for i, c in chunks_at(n):
                        if by_act(i, c):
                            pt_copy(act, lambda o, x: A(o, x, ACT.Copy), pair, i)
                    fronts_at(n, lambda name, u: front_part(name, pair, u + 1), order, fronts)

            def put_out(hf, full):
                act.wait_ge(ot_full, full)
                A(OS[:, hf, :, :], S[0:CH, hf, :].rearrange("p (c n) -> p c n", c=2), ACT.Copy).then_inc(os_made, 1)

            def pair_body(pair, p):
                attention(pair, 2)

            def group_tail(g):

                def put_z2(b, ab):
                    for k in range(4):
                        act.wait_ge(z2t_full, ab * 4 + (k + 1))
                        alone(act)
                        zv = ZP[k % 2].bitcast(F16).rearrange("p (j n) -> p j n", j=4)
                        A(Z2[:, b, k // 2, :, 256 * (k % 2):256 * (k % 2) + 256], zv[:, 0:3, :],
                          ACT.Copy).then_inc(z2t_made, 1)

                def abs_y1(ab):
                    for i in range(12):
                        act.wait_ge(y1_full, ab * 12 + (i + 1))
                        if i == 0:
                            act.wait_ge(max1_step, ab * 14 + (g + 1))
                        if i >= JR:
                            act.wait_ge(max1_step, ab * 14 + g + (i - JR + 2))
                        A(JUNK[:, i % JR, :], Y[i % 4], ACT.Abs, bias=B1[:, i % 6:i % 6 + 1]).then_inc(abs_made, 1)

                put_z2(0, g * GS)
                with act.Fori(0, GS - 1) as b:
                    ab = act.snap(g * GS + b)
                    abs_y1(ab)
                    put_z2(act.snap(b + 1), act.snap(ab + 1))
                abs_y1(g * GS + (GS - 1))

                def split_h(ab, i):
                    act.wait_ge(gelu_made, ab * 12 + (i + 1))
                    if i % MH == 0:
                        act.wait_ge(y2_full, ab * 4 + (2 * (i // MH) + 2))
                    A(HS[:, i // MH, 0, i % MH, :], H[:, i % MH, :], ACT.Copy).then_inc(hhi_made, 1)

                act.wait_ge(quant1_step, (g + 1) * 7)
                with act.Fori(0, GS) as b:
                    ab = act.snap(g * GS + b)
                    for i in range(12):
                        act.wait_ge(clip_made, ab * 12 + (i + 1))
                        h = H[:, i % MH, :]
                        A(h, h, ACT.Gelu, bias=rb1[:, i % 6:i % 6 + 1], scale=r1).then_inc(gelu_made, 1)
                        if i:
                            split_h(ab, i - 1)
                    split_h(ab, 2 * MH - 1)
                with act.Fori(0, GS) as b:
                    ab = act.snap(g * GS + b)
                    for hf in range(2):
                        act.wait_ge(stored[hf], ab * 16 + 16)
                        put_out(hf, ab * 2 + (hf + 3))
                for hf in range(2):
                    act.wait_ge(stored[hf], (g + 1) * (GS * 16) + 16)

            groups(act, pair_body, group_tail)
            attention(LAST, 1)
            for u in range(2):
                for hf in range(2):
                    act.wait_ge(stored[hf], 16 * (2 * LAST + u + 1))
                    put_out(hf, 4 * LAST + 2 * u + hf + 3)

        @block.vector
        def _(dve):
            v = nc.vector
            dve.wait_ge(w_in, 16 * 10)
            qk = W3f[:, :, 0:2 * C].rearrange("p j (m s d) -> p j m s d", m=3, s=2)
            kinds = (qk[:, :, :, 0, :], qk[:, :, :, 1, :], W3f[:, :, 2 * C:3 * C])
            for i, w in enumerate(kinds):
                v.tensor_reduce(sc[:, 33 + i:34 + i], w, AX.XY if i == 2 else AX.XYZ, ALU.max,
                                apply_absolute_value=True).then_inc(prep, 1)
            g1 = HID // NGROUPS
            g2 = C // NGROUPS
            for g in range(NGROUPS):
                v.tensor_reduce(sc[:, 36 + g:37 + g], W1f[:, :, g1 * g:g1 * g + g1], AX.XY, ALU.add).then_inc(prep, 1)
            for g in range(NGROUPS):
                v.tensor_reduce(sc[:, 41 + g:42 + g], W2f[:, :, g2 * g:g2 * g + g2], AX.XY, ALU.add).then_inc(prep, 1)
            chain = [3 + 2 * NGROUPS]

            def link(ins):
                chain[0] += 1
                ins.then_inc(prep, 1)
                dve.wait_ge(prep, chain[0])

            dve.wait_ge(prep_all, 1)
            v.memset(half, 0.5).then_inc(prep, 1)
            chain[0] += 1
            v.tensor_scalar(amax, amax, 1e-18, None, ALU.max).then_inc(prep, 1)
            chain[0] += 1
            dve.wait_ge(prep, chain[0])
            link(v.tensor_scalar(qkprod, amax[:, 0:1], amax[:, 1:2], 1.0 / (WTOP * WTOP * float(np.sqrt(C))),
                                 ALU.mult, ALU.mult))
            link(v.reciprocal(wscale, amax))
            link(v.tensor_scalar(wscale, wscale, WTOP, None, ALU.mult))
            link(v.tensor_scalar(vback, amax[:, 2:3], 1.0 / WTOP, None, ALU.mult))
            for i, w in enumerate(kinds):
                link(v.tensor_scalar(w, w, wscale[:, i:i + 1], None, ALU.mult))
            link(v.tensor_copy(W3h[:, :, :], W3f[:, :, :]))
            link(v.tensor_tensor(W3l[:, :, :], W3f[:, :, :], W3h[:, :, :], ALU.subtract))
            dve.wait_ge(prep_all, 2)
            link(v.tensor_scalar(sum1, sum1, 1.0 / (2 * g1 * C), None, ALU.mult))
            link(v.tensor_scalar(sum2, sum2, 1.0 / (g2 * HID), None, ALU.mult))
            link(v.memset(W1b[:, :, :], 0.0))
            link(v.memset(W2b[:, :, :], 0.0))
            for wf, wc, wbin, gs, means in ((W1f, W1c, W1b, g1, sum1), (W2f, W2c, W2b, g2, sum2)):
                for g in range(NGROUPS):
                    cols = slice(gs * g, gs * g + gs)
                    link(v.tensor_scalar(wc[:, :, cols], wf[:, :, cols], means[:, g:g + 1], None, ALU.is_lt))
                    link(v.scalar_tensor_tensor(out=wbin[:, :, cols], in0=wf[:, :, cols], scalar=means[:, g:g + 1],
                                                in1=wc[:, :, cols], op0=ALU.is_gt, op1=ALU.subtract))
            dve.wait_ge(prep_all, 3)
            dve.wait_ge(cst_made, 14)
            dve.wait_ge(bias_in, 16)
            v.memset(X[CH:CH + 1, 0, :], 1.0).then_inc(w_ready, 1)

            def layer_norm(src, step, step_base, rs_sem, rs_value, part, tiles=range(TT)):
                if part == "stats":
                    for t in tiles:
                        v.bn_stats(stats[:, t, :], src(t)).then_inc(step, 1)
                    for i, t in enumerate(tiles):
                        dve.wait_ge(step, step_base + (2 * tiles[0] + i + 1))
                        alone(dve)
                        v.bn_aggr(mv[:, t, :], stats[:, t, :]).then_inc(step, 1)
                elif part == "norm":
                    dve.wait_ge(rs_sem, rs_value)
                    for t in tiles:
                        v.tensor_scalar(Z[:, t, :], src(t), mv[:, t, 0:1], rstd[:, t:t + 1], ALU.subtract,
                                        ALU.mult).then_inc(step, 1)
                else:
                    dve.wait_ge(step, step_base + 16 + tiles[-1] + 1)
                    ts = slice(tiles[0], tiles[-1] + 1)
                    v.tensor_copy(zcat[:, ts, 0:C], Z[:, ts, :]).then_inc(step, 1)

            def front_part(name, pair, u):
                f = u % 2
                step = {"norms": "na", "logits": "rb"}.get(name, name)
                FR, free = (FB[bank_of(step)], front_free[bank_of(step)]) if step in STEPS else (None, None)
                if name in ("wg0", "wg1"):
                    c, m = int(name[2]), CH + 1 - int(name[2])
                    if name == "wg0" and u:
                        for st in stacked:
                            dve.wait_ge(st, after(pair, u, STACKS, 0))
                    dve.wait_ge(front_full, after(pair, u, FRONT_STEPS, STEPS.index(name) + 1))
                    v.tensor_tensor(PROD[0:m, c, :], FR[0:m, 0:2 * C], WT[0:m, c, :], ALU.mult).then_inc(free, 1)
                elif name == "norms":
                    dve.wait_ge(front_full, after(pair, u, FRONT_STEPS, STEPS.index("na") + 1))
                    v.tensor_scalar(NK[:, :], FR[0:CH, C:C + 4], NORM_EPS2, None, ALU.max).then_inc(norm2_made, 1)
                    v.tensor_copy(LOG, FR[0:CH, 256:256 + C].rearrange("p (a b) -> p a b", a=2)).then_inc(free, 1)
                elif name == "rdiag":
                    dve.wait_ge(rnorm_made, after(pair, u, 1, 1))
                    v.tensor_tensor(RD[:, :, :], ident[0:CH, 0:CH].unsqueeze(1).broadcast_to([CH, 2, CH]),
                                    NK[:, 2:4].unsqueeze(2).broadcast_to([CH, 2, CH]), ALU.mult).then_inc(xsoft, 1)
                    v.tensor_tensor(rqt, NK[:, 0:2], tempc[:, :], ALU.mult).then_inc(xsoft, 1)
                elif name == "logits":
                    dve.wait_ge(front_full, after(pair, u, FRONT_STEPS, STEPS.index("rb") + 1))
                    dve.wait_ge(xsoft, after(pair, u, XSOFT, 2))
                    for j in range(2):
                        v.scalar_tensor_tensor(out=LOG[:, j, :], in0=LOG[:, j, :], scalar=rqt[:, j:j + 1],
                                               in1=FR[0:CH, CH * j:CH * j + CH],
                                               op0=ALU.mult, op1=ALU.mult).then_inc(xsoft, 1)
                    dve.wait_ge(xsoft, after(pair, u, XSOFT, 4))
                    v.tensor_tensor(LOG, LOG, blockmask[:, :, :], ALU.add).then_inc(xsoft, 1)
                    dve.wait_ge(xsoft, after(pair, u, XSOFT, 5))
                    dve.sem_inc(free, 1)
                    v.tensor_reduce(xmax, LOG, AX.X, ALU.max, negate=True).then_inc(xsoft, 1)
                elif name == "attn":
                    dve.wait_ge(xexp_made, after(pair, u, 2, 2))
                    v.reciprocal(xrec, xsum).then_inc(xsoft, 1)
                    dve.wait_ge(xsoft, after(pair, u, XSOFT, 7))
                    for j in range(2):
                        v.tensor_scalar(ATT[:, j, :], ATT[:, j, :], xrec[:, j:j + 1], None,
                                        ALU.mult).then_inc(xsoft, 1)
                elif name == "mt":
                    dve.wait_ge(front_full, after(pair, u, FRONT_STEPS, STEPS.index("mt") + 1))
                    for c in range(2):
                        m = CH + 1 - c
                        v.tensor_tensor(MT[0:m, c, :], FR[0:m, C * c:C * c + C], IADD[0:m, c, :],
                                        ALU.add).then_inc(free, 1)
                elif name.startswith("ln"):
                    tiles = range(4, 8) if name.endswith("1") else range(4)
                    if name.startswith("ln_stats"):
                        for t in tiles[0] // 2, tiles[2] // 2:
                            wait_freed(dve, pair, u, f"t{t}")
                    layer_norm(lambda t: T0[:, f, t, :], ln_step, after(pair, u, LN_PER, 0), rstd_made,
                               after(pair, u, 2, 2), name[3:].rstrip("01"), tiles)
                elif name.startswith("qk"):
                    i = int(name[2:])
                    dve.wait_ge(qkhi_made, after(pair, u, 6, i + 1))
                    cols = slice(512 * (i % 2), 512 * (i % 2) + 512)
                    v.scalar_tensor_tensor(out=QKL[:, i // 2, cols], in0=FR, scalar=qkback,
                                           in1=QKH[:, i // 2, cols], op0=ALU.mult,
                                           op1=ALU.subtract).then_inc(qklo_made, 1)
                    dve.wait_ge(qklo_made, after(pair, u, 6, i + 1))
                    dve.sem_inc(free, 1)

            order = list(SLOTS.items()) + [a for a in SMALL_SLOTS.items() if a[0] != "xexp"]
            order.sort(key=lambda a: a[1])
            for name, _ in order:
                front_part(name, 0, 0)
            later = sorted([(name, at + name.startswith("qk")) for name, at in order], key=lambda a: a[1])

            def add_to_t1(pair, slot, i, k):
                base = of_pair(pair, 3 * K2, 3 * k)
                dve.wait_ge(pt_full[i % 2], of_pair(pair, PT_PER, i // 2 + 1))
                v.reciprocal(rsum3, rowsum[:, unit_of(k, 0):unit_of(k, 2) + 1:2]).then_inc(t1_step, 1)
                dve.wait_ge(t1_step, base + 1)
                v.tensor_tensor(fin[:, :].rearrange("p (h d) -> p h d", h=3),
                                PT[i % 2][:, 0:CH].rearrange("p (h d) -> p h d", h=3),
                                rsum3[:, 0:3].unsqueeze(2).broadcast_to([P, 3, D]), ALU.mult).then_inc(t1_step, 1)
                dve.wait_ge(t1_step, base + 2)
                dve.sem_inc(pt_free[i % 2], 1)
                u, qt, grp = k // (K2 // 2), qtile(unit_of(k, 0)), k % (K2 // 2) // 8
                cols = slice(CH * grp, CH * grp + CH)
                v.tensor_tensor(T1[:, slot + u, qt, cols], fin[:, :], T0[:, u, qt, cols], ALU.add).then_inc(t1_step, 1)

            def attention(pair, fronts, slot):
                for n in range(LAST_SLOT + 2):
                    if n < U2:
                        dve.wait_ge(scores_full, of_pair(pair, U2, n + 1))
                        v.tensor_reduce(nmax[:, n:n + 1], S[:, n % 2, 0:P * (qtile(n) + 1)], AX.X, ALU.max,
                                        negate=True).then_inc(max_made, 1)
                    for i, c in chunks_at(n):
                        if c[1] == "p" and not by_act(i, c):
                            pt_copy(dve, v.tensor_copy, pair, i)
                    for i, c in chunks_at(n):
                        if c[1] == "o":
                            add_to_t1(pair, slot, i, c[2])
                    fronts_at(n, lambda name, u: front_part(name, pair, u + 1), later, fronts)

            def pair_body(pair, p):
                attention(pair, 2, p * 2)

            def group_tail(g):
                nb = g + 1
                for st in stacked:
                    dve.wait_ge(st, nb * (GS * STACKS) + STACKS)
                v.memset(run1, 0.0).then_inc(max1_step, 1)

                def norm2(b, ab, part, tiles):
                    layer_norm(lambda t: T1[:, b, t, :], ln2_step, ab * LN_PER, rstd2_made, ab * 2 + 2, part, tiles)

                def max_y1(ab, first, last):
                    for i in range(first, last):
                        dve.wait_ge(abs_made, ab * 12 + (i + 1))
                        v.tensor_reduce(gm[:, i:i + 1], JUNK[:, i % JR, :], AX.X, ALU.max).then_inc(max1_step, 1)
                    if last == 12:
                        base = ab * 14 + (g + 1)
                        dve.wait_ge(max1_step, base + 12)
                        v.tensor_reduce(gm[:, 12:13], gm[:, 0:12], AX.X, ALU.max).then_inc(max1_step, 1)
                        dve.wait_ge(max1_step, base + 13)
                        v.tensor_tensor(run1, run1, gm[:, 12:13], ALU.max).then_inc(max1_step, 1)

                halves = (range(4), range(4, 8))
                for part, tiles in (("stats", range(TT)), ("norm", range(TT)), ("round", halves[0]), ("round", halves[1])):
                    norm2(0, g * GS, part, tiles)
                with dve.Fori(0, GS - 1) as b:
                    ab = dve.snap(g * GS + b)
                    b1, ab1 = dve.snap(b + 1), dve.snap(ab + 1)
                    dve.wait_ge(z2t_full, ab * 4 + 4)
                    alone(dve)
                    norm2(b1, ab1, "stats", range(TT))
                    max_y1(ab, 0, 4)
                    norm2(b1, ab1, "norm", range(TT))
                    norm2(b1, ab1, "round", halves[0])
                    norm2(b1, ab1, "round", halves[1])
                    max_y1(ab, 4, 12)
                max_y1(g * GS + (GS - 1), 0, 12)
                dve.wait_ge(gam1_made, nb)
                q0 = g * 7
                v.tensor_scalar(ge, gam1, Q_EPS, None, ALU.add).then_inc(quant1_step, 1)
                dve.wait_ge(quant1_step, q0 + 1)
                v.reciprocal(gr, ge).then_inc(quant1_step, 1)
                v.tensor_scalar(c1, ge, (QB - Q_EPS) / QB, None, ALU.mult).then_inc(quant1_step, 1)
                dve.wait_ge(quant1_step, q0 + 2)
                v.tensor_scalar(r1, gr, QB, None, ALU.mult).then_inc(quant1_step, 1)
                dve.wait_ge(quant1_step, q0 + 4)
                v.tensor_scalar(clip_hi, B1[:, :], -1.0, c1, ALU.mult, ALU.add).then_inc(quant1_step, 1)
                v.tensor_scalar(clip_lo, B1[:, :], -1.0, c1, ALU.mult, ALU.subtract).then_inc(quant1_step, 1)
                v.tensor_scalar(rb1, B1[:, :], r1, None, ALU.mult).then_inc(quant1_step, 1)
                dve.wait_ge(quant1_step, q0 + 7)
                v.memset(run2, 0.0).then_inc(max2_step, 1)

                def clip_y(ab, hf):
                    for i in range(MH * hf, MH * hf + MH):
                        dve.wait_ge(y_full, ab * 12 + (i + 1))
                        dve.wait_ge(hlo_made, ab * 12 + (i + 1))
                        m = i % MH
                        v.tensor_scalar(H[:, m, :], Y[i % 4], clip_hi[:, m:m + 1], clip_lo[:, m:m + 1],
                                        ALU.min, ALU.max).then_inc(clip_made, 1)

                def put_y2(b, ab, hf):
                    for tp in range(2 * hf, 2 * hf + 2):
                        dve.wait_ge(y2_full, ab * 4 + (tp + 5))
                        o = 2 * C * (tp % 2)
                        v.tensor_tensor(Y2[:, b, tp // 2, o:o + 2 * C].rearrange("p (a c) -> p a c", a=2),
                                        PT[tp % 2][:, 0:2 * C].rearrange("p (a c) -> p a c", a=2),
                                        B2[:, :].unsqueeze(1).broadcast_to([P, 2, C]), ALU.add).then_inc(y2_made, 1)

                def max_y2(b, ab, hf):
                    base = ab * 4 + (g + 1)
                    dve.wait_ge(y2_made, ab * 4 + (2 * hf + 2))
                    alone(dve)
                    v.tensor_reduce(gm[:, 13:14], Y2[:, b, hf], AX.X, ALU.max,
                                    apply_absolute_value=True).then_inc(max2_step, 1)
                    dve.wait_ge(max2_step, base + (2 * hf + 1))
                    v.tensor_tensor(run2, run2, gm[:, 13:14], ALU.max).then_inc(max2_step, 1)

                clip_y(g * GS, 0)
                with dve.Fori(0, GS - 1) as b:
                    ab = dve.snap(g * GS + b)
                    clip_y(ab, 1)
                    put_y2(b, ab, 0)
                    clip_y(dve.snap(ab + 1), 0)
                    max_y2(b, ab, 0)
                    put_y2(b, ab, 1)
                    max_y2(b, ab, 1)
                ab = g * GS + (GS - 1)
                clip_y(ab, 1)
                put_y2(GS - 1, ab, 0)
                max_y2(GS - 1, ab, 0)
                put_y2(GS - 1, ab, 1)
                max_y2(GS - 1, ab, 1)
                dve.wait_ge(gam2_made, nb)
                q0 = g * 5
                v.tensor_scalar(ge2, gam2, Q_EPS, None, ALU.add).then_inc(quant2_step, 1)
                dve.wait_ge(quant2_step, q0 + 1)
                v.reciprocal(gr2, ge2).then_inc(quant2_step, 1)
                v.tensor_scalar(c2, ge2, (QB - Q_EPS) / QB, None, ALU.mult).then_inc(quant2_step, 1)
                v.tensor_scalar(c2n, ge2, -(QB - Q_EPS) / QB, None, ALU.mult).then_inc(quant2_step, 1)
                dve.wait_ge(quant2_step, q0 + 4)
                v.tensor_scalar(r2, gr2, QB, None, ALU.mult).then_inc(quant2_step, 1)
                dve.wait_ge(quant2_step, q0 + 5)
                alone(dve)
                with dve.Fori(0, GS) as b:
                    ab = dve.snap(g * GS + b)
                    for hf in range(2):
                        dve.wait_ge(ot_full, ab * 2 + (hf + 1))
                        v.tensor_scalar(OT[:, hf, :], Y2[:, b, hf, :], c2, c2n, ALU.min, ALU.max).then_inc(o_step, 1)
                    for hf in range(2):
                        dve.wait_ge(o_step, ab * 4 + (hf + 1))
                        v.scalar_tensor_tensor(out=OT[:, hf, :], in0=OT[:, hf, :], scalar=r2, in1=T1H[:, b, hf, :],
                                               op0=ALU.mult, op1=ALU.add).then_inc(o_step, 1)

            groups(dve, pair_body, group_tail)
            attention(LAST, 1, 0)


def kernel(x, L0_conv_w_qkv, L0_conv_b_qkv, L0_conv_temperature, L0_conv_w_proj, L0_conv_b_proj, L1_attn_Wq,
           L1_attn_Wk, L1_attn_Wv, L1_ffn_W1, L1_ffn_b1, L1_ffn_W2, L1_ffn_b2):
    import concourse.bacc as bacc
    from concourse.bass_utils import run_bass_kernel_spmd as run

    (x, wqkv, bqkv, temp, wp, bp, wq, wk, wv, w1, b1, w2, b2) = [np.asarray(a) for a in (
        x, L0_conv_w_qkv, L0_conv_b_qkv, L0_conv_temperature, L0_conv_w_proj, L0_conv_b_proj, L1_attn_Wq,
        L1_attn_Wk, L1_attn_Wv, L1_ffn_W1, L1_ffn_b1, L1_ffn_W2, L1_ffn_b2)]
    B = x.shape[0]
    wt = wqkv.T
    stack = lambda a: np.concatenate([a, a], 0).reshape(3, P, -1).transpose(1, 0, 2)
    v_rows, v_bias = wqkv[2 * C:3 * C], bqkv[2 * C:3 * C][:, None]
    arrays = {
        "x": x.reshape(B, C, NTOK),
        "wa": np.concatenate([wt[0:CH, 0:2 * C], bqkv[None, 0:2 * C]], 0),
        "wb": wt[CH:C, 0:2 * C],
        "wv": np.concatenate([v_rows[:, 0:CH], v_bias, v_rows[:, CH:C]], 1).reshape(2, CH, C + 1).transpose(1, 0, 2),
        "wpt": wp.T.reshape(2, CH, C).transpose(1, 0, 2),
        "bp": bp[None, :],
        "temp": np.repeat(temp.reshape(XH), XD).reshape(2, CH).T,
        "w3": stack(np.concatenate([w[:, D * h:D * h + D] for m in range(3) for w in (wq, wk) for h in (m, 3 + m)]
                                   + [wv], 1)),
        "w1": stack(w1.T),
        "b1": b1.reshape(MH, P).T,
        "w2": w2.T.reshape(MH, P, C).transpose(1, 0, 2),
        "b2": np.broadcast_to(b2, (P, C)),
    }
    arrays = {f"in_{k}": np.ascontiguousarray(a) for k, a in arrays.items()}
    nc = bacc.Bacc("TRN2", target_bir_lowering=False, num_devices=1)
    args = [nc.dram_tensor(k, a.shape, F32, kind="ExternalInput").ap() for k, a in arrays.items()]
    out = nc.dram_tensor("out_y", (B, C, NTOK), F32, kind="ExternalOutput").ap()
    hybrid_kernel(nc, *args, out)
    r = run(nc, [arrays], core_ids=[0])
    return r.results[0]["out_y"].reshape(x.shape)
```
